# Optimizing a Trainium2 kernel written in Bass

```python
import numpy as np
import jax
import jax.numpy as jnp

def _softmax(x, axis=-1):
    return jax.nn.softmax(x, axis=axis)

def _gelu(x):
    return jax.nn.gelu(x, approximate=True)

def _silu(x):
    return jax.nn.silu(x)

def _sigmoid(x):
    return jax.nn.sigmoid(x)

def _layernorm(x, axis=-1, eps=1e-05):
    m = jnp.mean(x, axis=axis, keepdims=True)
    v = jnp.var(x, axis=axis, keepdims=True)
    return (x - m) / jnp.sqrt(v + eps)

def _scatter_add(tgt, idx, src, axis=0):
    return tgt.at[idx].add(src)

def _segment_sum(src, seg, n):
    return jax.ops.segment_sum(src, seg, n)
kernel_name = 'mk_early_fusion_embed_d1_tok_img1024_r4_62ab1b'

def setup_inputs(seed: int=0):
    np.random.seed(seed)
    _w = jnp.asarray

    def _rec_inputs():
        import jax
        import jax.numpy as jnp
        _rk = jax.random.key(seed)
        x = -0.00150118 + 0.499729 * jax.random.normal(jax.random.fold_in(_rk, 1), (16, 256, 64, 2), jnp.float32)
        x_txt = jax.random.randint(jax.random.fold_in(_rk, 51), (16, 128), 0, 12564, jnp.int32)
        return (x, x_txt)
    x, x_txt = _rec_inputs()

    def _L0_tok_setup():
        import jax, jax.numpy as jnp
        import numpy as np
        import math
        H = 256
        N = 64
        CH = 1
        SEQ_L = 256
        key = jax.random.key(seed)
        k1, k2, k3, k4 = jax.random.split(key, 4)
        log_dt = jax.random.uniform(k1, (H,), dtype=jnp.float32, minval=math.log(0.001), maxval=math.log(0.1))
        inv_A_real = jnp.log(0.5 * jnp.ones((H, N), jnp.float32)) + 0.1 * jax.random.normal(k2, (H, N), dtype=jnp.float32)
        A_imag = jnp.broadcast_to(math.pi * jnp.arange(N, dtype=jnp.float32), (H, N)).copy()
        B_ri = jax.random.normal(k3, (H, N, 2), dtype=jnp.float32) * 0.5
        C_ri = jax.random.normal(k4, (CH, H, N, 2), dtype=jnp.float32) * 0.5
        return {'log_dt': log_dt, 'inv_A_real': inv_A_real, 'A_imag': A_imag, 'B_ri': B_ri, 'C_ri': C_ri, 'L': SEQ_L}
    _L0_tok_all = _L0_tok_setup()
    _L0_tok_in = {k: v for k, v in _L0_tok_all.items() if k in ('log_dt', 'inv_A_real', 'A_imag', 'B_ri')}
    del _L0_tok_all

    def _L0_txt_setup():
        import jax, jax.numpy as jnp
        import numpy as np
        VOCAB = 50257
        HIDDEN = 256
        key = jax.random.key(seed)
        k1, k2, k3 = jax.random.split(key, 3)
        seq = jax.random.randint(k1, (8, 1024), 0, VOCAB, dtype=jnp.int64 if jax.config.jax_enable_x64 else jnp.int32)
        bound = 1.0 / np.sqrt(VOCAB)
        W = jax.random.uniform(k2, (HIDDEN, VOCAB), jnp.float32, -bound, bound)
        b = jax.random.uniform(k3, (HIDDEN,), jnp.float32, -bound, bound)
        return {'seq': seq, 'W': W, 'b': b}
    _L0_txt_all = _L0_txt_setup()
    _L0_txt_in = {k: v for k, v in _L0_txt_all.items() if k in ('W', 'b')}
    del _L0_txt_all

    def _L0_attn_setup():
        import jax, jax.numpy as jnp
        import numpy as np
        import math
        B, T, D = (2, 512, 256)
        N_HEADS = 16
        D_HEAD = D // N_HEADS

        def _rope_tables(t, d_head, dtype=jnp.float32):
            theta = 1.0 / 10000.0 ** (jnp.arange(0, d_head, 2, dtype=jnp.float32) / d_head)
            angles = jnp.outer(jnp.arange(t, dtype=jnp.float32), theta)
            angles = jnp.concatenate([angles, angles], axis=-1)
            return (jnp.cos(angles).astype(dtype), jnp.sin(angles).astype(dtype))

        def _rotate_half(x):
            half = x.shape[-1] // 2
            return jnp.concatenate([-x[..., half:], x[..., :half]], axis=-1)

        def _apply_rope(x, cos, sin):
            return x * cos[None, None] + _rotate_half(x) * sin[None, None]
        key = jax.random.key(seed)
        k1, k2, k3, k4 = jax.random.split(key, 4)
        s_in = 1.0 / math.sqrt(D)
        return {'x': jax.random.normal(k1, (B, T, D), dtype=jnp.float32), 'w_qkv': jax.random.normal(k2, (D, 3 * D), dtype=jnp.float32) * s_in, 'w_out': jax.random.normal(k3, (D, D), dtype=jnp.float32) * s_in, 'b_out': jax.random.normal(k4, (D,), dtype=jnp.float32) * 0.01}
    _L0_attn_all = _L0_attn_setup()
    _L0_attn_in = {k: v for k, v in _L0_attn_all.items() if k in ('w_qkv', 'w_out', 'b_out')}
    del _L0_attn_all

    def _L0_ffn_setup():
        import jax, jax.numpy as jnp
        import numpy as np
        DIM = 256
        EXPERT_DIM = 128
        N_EXPERTS = 16
        TOPK = 2
        SHARED_HIDDEN = EXPERT_DIM * TOPK
        B, T = (4, 256)

        def _moe_forward(x, router_w, router_bias, up_proj, gate_proj, down_proj, sh_gate, sh_up, sh_down):
            Bb, Tt, D = x.shape
            flat = x.reshape(Bb * Tt, D)
            N = flat.shape[0]
            logits = flat @ router_w.T
            topk_scores, topk_idx = jax.lax.top_k(logits + router_bias, TOPK)
            topk_scores = jax.nn.softmax(topk_scores, axis=-1)
            combine = jnp.zeros((N, N_EXPERTS), flat.dtype)
            combine = combine.at[jnp.arange(N)[:, None], topk_idx].add(topk_scores)
            up_all = jnp.einsum('nd,kde->nke', flat, up_proj)
            gate_all = jnp.einsum('nd,kde->nke', flat, gate_proj)
            hidden = jax.nn.silu(gate_all) * up_all
            down_all = jnp.einsum('nke,ked->nkd', hidden, down_proj)
            out = jnp.einsum('nk,nkd->nd', combine, down_all)
            sh_hidden = jax.nn.silu(flat @ sh_gate.T) * (flat @ sh_up.T)
            out = out + sh_hidden @ sh_down.T
            return out.reshape(Bb, Tt, D)
        key = jax.random.key(seed)
        ks = jax.random.split(key, 9)
        std = 0.02
        return {'x': jax.random.normal(ks[0], (B, T, DIM), jnp.float32), 'router_w': jax.random.normal(ks[1], (N_EXPERTS, DIM), jnp.float32) * std, 'router_bias': jnp.zeros((N_EXPERTS,), jnp.float32), 'up_proj': jax.random.normal(ks[2], (N_EXPERTS, DIM, EXPERT_DIM), jnp.float32) * std, 'gate_proj': jax.random.normal(ks[3], (N_EXPERTS, DIM, EXPERT_DIM), jnp.float32) * std, 'down_proj': jax.random.normal(ks[4], (N_EXPERTS, EXPERT_DIM, DIM), jnp.float32) * std, 'sh_gate': jax.random.normal(ks[5], (SHARED_HIDDEN, DIM), jnp.float32) * std, 'sh_up': jax.random.normal(ks[6], (SHARED_HIDDEN, DIM), jnp.float32) * std, 'sh_down': jax.random.normal(ks[7], (DIM, SHARED_HIDDEN), jnp.float32) * std}
    _L0_ffn_all = _L0_ffn_setup()
    _L0_ffn_in = {k: v for k, v in _L0_ffn_all.items() if k in ('router_w', 'router_bias', 'up_proj', 'gate_proj', 'down_proj', 'sh_gate', 'sh_up', 'sh_down')}
    del _L0_ffn_all
    return {'x': x, 'x_txt': x_txt, 'L0_tok_log_dt': _L0_tok_in['log_dt'], 'L0_tok_inv_A_real': _L0_tok_in['inv_A_real'], 'L0_tok_A_imag': _L0_tok_in['A_imag'], 'L0_tok_B_ri': _L0_tok_in['B_ri'], 'L0_txt_W': _L0_txt_in['W'], 'L0_txt_b': _L0_txt_in['b'], 'L0_attn_w_qkv': _L0_attn_in['w_qkv'], 'L0_attn_w_out': _L0_attn_in['w_out'], 'L0_attn_b_out': _L0_attn_in['b_out'], 'L0_ffn_router_w': _L0_ffn_in['router_w'], 'L0_ffn_router_bias': _L0_ffn_in['router_bias'], 'L0_ffn_up_proj': _L0_ffn_in['up_proj'], 'L0_ffn_gate_proj': _L0_ffn_in['gate_proj'], 'L0_ffn_down_proj': _L0_ffn_in['down_proj'], 'L0_ffn_sh_gate': _L0_ffn_in['sh_gate'], 'L0_ffn_sh_up': _L0_ffn_in['sh_up'], 'L0_ffn_sh_down': _L0_ffn_in['sh_down']}

def reference(x, x_txt, L0_tok_log_dt, L0_tok_inv_A_real, L0_tok_A_imag, L0_tok_B_ri, L0_txt_W, L0_txt_b, L0_attn_w_qkv, L0_attn_w_out, L0_attn_b_out, L0_ffn_router_w, L0_ffn_router_bias, L0_ffn_up_proj, L0_ffn_gate_proj, L0_ffn_down_proj, L0_ffn_sh_gate, L0_ffn_sh_up, L0_ffn_sh_down):
    import jax
    import jax.numpy as jnp

    def _L0_tok_ref(log_dt, inv_A_real, A_imag, B_ri, C_ri, L):
        import jax, jax.numpy as jnp
        import numpy as np
        import math
        H = 256
        N = 64
        CH = 1
        SEQ_L = 256
        dt = jnp.exp(log_dt)
        A = -jnp.exp(inv_A_real) + 1j * A_imag
        B = B_ri[..., 0] + 1j * B_ri[..., 1]
        C = C_ri[..., 0] + 1j * C_ri[..., 1]
        dtA = A * dt[:, None]
        dA = (1.0 + dtA / 2) / (1.0 - dtA / 2)
        C_term = C * B[None]
        log_dA = jnp.log(dA)
        V = jnp.exp(log_dA[:, :, None] * jnp.arange(L))
        K = 2.0 * jnp.einsum('chn,hnl->chl', C_term, V).real
        return K.astype(jnp.float32)

    def _L0_txt_ref(seq, W, b):
        import jax, jax.numpy as jnp
        import numpy as np
        VOCAB = 50257
        HIDDEN = 256
        out = jnp.take(W, seq, axis=1)
        out = jnp.moveaxis(out, 0, -1) + b
        return out

    def _L0_attn_ref(x, w_qkv, w_out, b_out):
        import jax, jax.numpy as jnp
        import numpy as np
        import math
        B, T, D = (2, 512, 256)
        N_HEADS = 16
        D_HEAD = D // N_HEADS

        def _rope_tables(t, d_head, dtype=jnp.float32):
            theta = 1.0 / 10000.0 ** (jnp.arange(0, d_head, 2, dtype=jnp.float32) / d_head)
            angles = jnp.outer(jnp.arange(t, dtype=jnp.float32), theta)
            angles = jnp.concatenate([angles, angles], axis=-1)
            return (jnp.cos(angles).astype(dtype), jnp.sin(angles).astype(dtype))

        def _rotate_half(x):
            half = x.shape[-1] // 2
            return jnp.concatenate([-x[..., half:], x[..., :half]], axis=-1)

        def _apply_rope(x, cos, sin):
            return x * cos[None, None] + _rotate_half(x) * sin[None, None]
        b, t, d = x.shape
        qkv = x @ w_qkv
        qkv = qkv.reshape(b, t, 3, N_HEADS, D_HEAD)
        q = jnp.transpose(qkv[:, :, 0], (0, 2, 1, 3))
        k = jnp.transpose(qkv[:, :, 1], (0, 2, 1, 3))
        v = jnp.transpose(qkv[:, :, 2], (0, 2, 1, 3))
        cos, sin = _rope_tables(t, D_HEAD, x.dtype)
        q = _apply_rope(q, cos, sin)
        k = _apply_rope(k, cos, sin)
        scores = jnp.einsum('bhqd,bhkd->bhqk', q, k) / math.sqrt(D_HEAD)
        probs = jax.nn.softmax(scores, axis=-1)
        out = jnp.einsum('bhqk,bhkd->bhqd', probs, v)
        out = jnp.transpose(out, (0, 2, 1, 3)).reshape(b, t, d)
        return out @ w_out + b_out

    def _L0_ffn_ref(x, router_w, router_bias, up_proj, gate_proj, down_proj, sh_gate, sh_up, sh_down):
        import jax, jax.numpy as jnp
        import numpy as np
        DIM = 256
        EXPERT_DIM = 128
        N_EXPERTS = 16
        TOPK = 2
        SHARED_HIDDEN = EXPERT_DIM * TOPK
        B, T = (4, 256)

        def _moe_forward(x, router_w, router_bias, up_proj, gate_proj, down_proj, sh_gate, sh_up, sh_down):
            Bb, Tt, D = x.shape
            flat = x.reshape(Bb * Tt, D)
            N = flat.shape[0]
            logits = flat @ router_w.T
            topk_scores, topk_idx = jax.lax.top_k(logits + router_bias, TOPK)
            topk_scores = jax.nn.softmax(topk_scores, axis=-1)
            combine = jnp.zeros((N, N_EXPERTS), flat.dtype)
            combine = combine.at[jnp.arange(N)[:, None], topk_idx].add(topk_scores)
            up_all = jnp.einsum('nd,kde->nke', flat, up_proj)
            gate_all = jnp.einsum('nd,kde->nke', flat, gate_proj)
            hidden = jax.nn.silu(gate_all) * up_all
            down_all = jnp.einsum('nke,ked->nkd', hidden, down_proj)
            out = jnp.einsum('nk,nkd->nd', combine, down_all)
            sh_hidden = jax.nn.silu(flat @ sh_gate.T) * (flat @ sh_up.T)
            out = out + sh_hidden @ sh_down.T
            return out.reshape(Bb, Tt, D)
        return _moe_forward(x, router_w, router_bias, up_proj, gate_proj, down_proj, sh_gate, sh_up, sh_down)
    h = _L0_tok_ref(L0_tok_log_dt, L0_tok_inv_A_real, L0_tok_A_imag, L0_tok_B_ri, x, 256)
    h = jnp.concatenate([h, _L0_txt_ref(x_txt, L0_txt_W, L0_txt_b)], axis=1)
    h = h + _L0_attn_ref(_layernorm(h, axis=-1), L0_attn_w_qkv, L0_attn_w_out, L0_attn_b_out)
    h = h + _L0_ffn_ref(_layernorm(h, axis=-1), L0_ffn_router_w, L0_ffn_router_bias, L0_ffn_up_proj, L0_ffn_gate_proj, L0_ffn_down_proj, L0_ffn_sh_gate, L0_ffn_sh_up, L0_ffn_sh_down)
    return h

_drawn_inputs = setup_inputs


def setup_inputs(seed=0):
    import zlib

    import numpy as np

    out = dict(_drawn_inputs(seed))
    spreads = {'L0_ffn_router_bias': (0.0, 0.8)}
    factors = {'L0_txt_W': 6.206,
     'L0_attn_b_out': 8.0,
     'L0_ffn_router_w': 8.0,
     'L0_ffn_up_proj': 8.0,
     'L0_ffn_gate_proj': 8.0,
     'L0_ffn_down_proj': 8.0,
     'L0_ffn_sh_gate': 8.0,
     'L0_ffn_sh_up': 8.0,
     'L0_ffn_sh_down': 8.0}
    for name, (base, spread) in spreads.items():
        noise = np.random.default_rng([zlib.crc32(name.encode()), seed]).standard_normal(out[name].shape)
        drawn = base * np.exp(spread * noise) if base else spread * noise
        out[name] = jnp.asarray(drawn.astype(out[name].dtype))
    for name, factor in factors.items():
        out[name] = (out[name] * factor).astype(out[name].dtype)
    return out
```

```python
import concourse.bass as bass
from concourse import mybir
from contextlib import ExitStack
import math

P = 128
NB = 16
D = 256
NS = 256
N = 64
NT = 128
T = NS + NT
TT = T // P
VOCAB = 50257
NH, DH = 16, 16
QW = 64
MROW = 48
NE = 16
ED = 128
EPS = 1e-5
SPLIT = -4096
LOG2E = 1.4426950408889634
ROUND = 12582912.0
LN2_HI, LN2_LO = 0.693359375, -2.12194440e-4
EXP_TERMS = 7
MAGIC = 1597463007.0
LA = 4
LB = D // LA
HC = 32
NCH = P // HC
SP_TOK = 56
SP_LEAD = 16
TU = 8

TOPK = 2
SLOTS = TT * TOPK
REG = NB * T + P
XROWS = NE * REG + P
NTILE = NB * T * TOPK // P + NE
ROWS_AT = 9
TG = 4
PAR_STEPS = 30
WT_STEP = PAR_STEPS + 1
POST_STEPS = 23
OUT_STEPS = 3 + 20 + 6 + 2 + 5
LN_STEPS = 20 + 1

F_READS = [1, 1] + [3, 1] * 3 + [1, 1, 2, 2] * 3
O_READS = [1] * 13 + [7] + [1] * 4
X_USE, QKV_USE, SPLIT_USE = 0, 2, 8
NORM_USE, ATT_USE, PROJ_USE, X2_USE, ROUTE_USE, FFN_USE, RANK_USE, DOWN_USE = 0, 3, 5, 8, 10, (11, 14), 13, 16


def reads(uses, u, n):
    return sum(uses[n:u:2])


def val(b, per, c, step=2):
    i, off = b
    return off * per + c if i is None else i * (step * per) + (off * per + c)


def is_batch(b, n):
    return b[0] is None and b[1] == n


def batch_index(b):
    i, off = b
    return off if i is None else i * 2 + off


def half(b, per):
    i, off = b
    return (off // 2 + 1) * per if i is None else i * per + (off // 2 + 1) * per


class Steps:

    def __init__(self, eng, sem, per):
        self.eng, self.sem, self.per = eng, sem, per

    def start(self, b):
        self.b, self.k = b, 0

    def add(self, ins):
        self.k += 1
        ins.then_inc(self.sem, 1)

    def done(self):
        self.eng.wait_ge(self.sem, val(self.b, self.per, self.k))

    def __call__(self, ins):
        self.add(ins)
        self.done()

    def end(self):
        assert self.k == self.per, (self.k, self.per)


def build(nc, x, x_txt, log_dt, inv_A_real, A_imag, B_ri, txt_W, txt_b, w_qkv, w_out, b_out,
          router_w, router_bias, up_proj, gate_proj, down_proj, sh_gate, sh_up, sh_down,
          rope_cos, rope_sin, identity, prefix, expert_rows, out):
    f32, f32r, i32, u32 = mybir.dt.float32, mybir.dt.float32r, mybir.dt.int32, mybir.dt.uint32
    ALU, ACT, AX = mybir.AluOpType, mybir.ActivationFunctionType, mybir.AxisListType
    V, S, PE = nc.vector, nc.scalar, nc.tensor

    ctx = ExitStack()
    with ctx:
        def sb(name, shape, dt=f32):
            return ctx.enter_context(nc.sbuf_tensor(name, shape, dt))

        def sem(name):
            return ctx.enter_context(nc.semaphore(name))

        text_d = nc.dram_tensor("text_d", (NB * NT, D), f32, kind="Internal").ap()
        x_d = nc.dram_tensor("x_d", (XROWS, D), f32, kind="Internal").ap()
        y_d = nc.dram_tensor("y_d", (NTILE * P, D), f32, kind="Internal").ap()
        h2_d = nc.dram_tensor("h2_d", (NB, T, D), f32, kind="Internal").ap()
        kern_d = nc.dram_tensor("kern_d", (P, 2, NB, D), f32, kind="Internal").ap()

        ident = sb("ident", [P, P])
        wqkv = sb("wqkv", [P, 2, 3 * D])
        wout = sb("wout", [P, 2, D])
        shg_t, shu_t, shd_t = (sb(n, [P, 2, D]) for n in ("shg_t", "shu_t", "shd_t"))
        rw_t = sb("rw_t", [P, 2, NE])
        cos = sb("cos", [P, TT, 2, DH])
        sin = sb("sin", [P, TT, 2, DH])
        bout = sb("bout", [P, D])
        btxt = sb("btxt", [P, D])
        rbias = sb("rbias", [P, NE])
        ids = sb("ids", [1, NB * NT], i32)
        topv = sb("topv", [P, NB * TT, 2])
        pos_all = sb("pos_all", [P, NB * SLOTS])
        ef_all = sb("ef_all", [P, NB * SLOTS])
        pfx = sb("pfx", [P, 2, P])
        erow = sb("erow", [P, 4, NE])
        tabc = sb("tabc", [P, 2])
        tab = sb("tab", [1, 2 * P], i32)
        ends = sb("ends", [P, NE], i32)
        pw = sb("pw", [P, NB * TT, TOPK])
        tv = sb("tv", [P, TT, 8])
        ti = sb("ti", [P, TT, 8], u32)

        gbuf = [sb(f"gbuf{n}", [P, TT, D]) for n in range(2)]
        hres = [sb(f"hres{n}", [P, TT, D]) for n in range(2)]
        xn = sb("xn", [P, TT, D])
        xnT = sb("xnT", [P, 2, T])
        attn = sb("attn", [P, TT, D])
        attnT = sb("attnT", [P, 2, T])
        h1 = sb("h1", [P, TT, D])
        xn2 = sb("xn2", [P, TT, D])
        xn2T = sb("xn2T", [P, 2, T])
        h2 = sb("h2", [P, TT, D])
        hid = sb("hid", [P, 2, T])
        ra = sb("ra", [P, 2 * NH, DH])
        rb = sb("rb", [P, 2 * NH, DH])
        rc = sb("rc", [P, 2 * NH, DH])
        tu, tg = (r[:, :, :].rearrange("p h d -> p (h d)")[:, 0:T] for r in (ra, rb))
        rs = sb("rs", [P, TT, NH])
        ef = sb("ef", [P, SLOTS])
        oh = sb("oh", [P, SLOTS, NE])
        rk = sb("rk", [P, SLOTS, NE])
        cum = sb("cum", [P, SLOTS + 1, NE])
        posf = sb("posf", [P, SLOTS])
        pos = sb("pos", [P, SLOTS], u32)
        lg = sb("lg", [P, TT, NE])
        bst = sb("bst", [P, TT, 6])
        mv = sb("mv", [P, TT, 2])
        nwt = sb("nwt", [P, 4, TT])
        factor, shift = sb("factor", [P, TT]), sb("shift", [P, TT])
        mx = sb("mx", [P, TT, 2, NH])
        mxT = sb("mxT", [2 * NH, T], f32r)
        pick = sb("pick", [2 * NH, NH], f32r)

        at = [0]

        def take(words, pattern, **kw):
            a = arena[:, at[0]:at[0] + words].rearrange(pattern, **kw)
            at[0] += words
            return a

        with nc.sbuf_tensor("ssm_arena", [P, 33024], f32) as arena:
            xin = take(NB * 2 * 2 * N, "p (c s w) -> p c s w", c=NB, s=2)
            CB = [take(NB * P, "p (c h) -> p c h", c=NB) for _ in range(2)]
            PW = take(9 * 2 * P, "p (k r h) -> p k r h", k=9, r=2)
            VV = [[take(HC * LB, "p (h b) -> p h b", h=HC) for _ in range(2)] for _ in range(2)]
            CC = [[take(HC * NB * LA, "p (h c a) -> p h c a", h=HC, c=NB) for _ in range(2)] for _ in range(2)]
            TM = [take(HC * LB // 2, "p (h b) -> p h b", h=HC) for _ in range(4)]
            KS = [take(512, "p (h b) -> p h b", h=8) for _ in range(4)]
            assert at[0] <= 33024
        weights_words = TT * 2 * NH * QW + 8 * T + NH * T
        with ExitStack() as attention:
            st = attention.enter_context(nc.sbuf_tensor("st", [P, TT, 2, NH, QW], f32))
            QT, KT, VP = [], [], []
            for n in range(2):
                QT.append(attention.enter_context(nc.sbuf_tensor(f"QT{n}", [P, 8, T], f32r)))
                KT.append(attention.enter_context(nc.sbuf_tensor(f"KT{n}", [P, NH, T], f32r)))
            for n in range(2):
                VP.append(attention.enter_context(nc.sbuf_tensor(f"VP{n}", [P, TT, NH, 32], f32)))
            EX = attention.enter_context(nc.sbuf_tensor("EX", [P, 6, T], f32))
            OT = attention.enter_context(nc.sbuf_tensor("OT", [P, 4, T], f32))
        arena = ctx.enter_context(nc.sbuf_tensor("moe_arena", [P, 33024], f32))
        at[0] = 0
        wgu = take(2 * NE * 2 * ED, "p (k m) -> p k m", k=2)
        wdn = take(NE * D, "p (m) -> p m")
        assert at[0] <= weights_words
        at[0] = weights_words
        xb = [take(D, "p (d) -> p d") for _ in range(TG)]
        yb = [take(D, "p (d) -> p d") for _ in range(TG)]
        xT = [take(D, "p (k t) -> p k t", k=2) for _ in range(2)]
        th, sg, hd, hT = ([take(ED, "p (e) -> p e") for _ in range(2)] for _ in range(4))
        ya = [[take(D, "p (d) -> p d") for _ in range(TOPK)] for _ in range(TG)]
        hb = [take(D, "p (d) -> p d") for _ in range(TG)]
        ob = [take(D, "p (d) -> p d") for _ in range(TG)]
        hb2 = [take(D, "p (d) -> p d") for _ in range(TG)]
        zero = take(D, "p (d) -> p d")
        ohall = take(NB * SLOTS * NE, "p (j e) -> p j e", e=NE)
        posy = take(NB * SLOTS, "p (j) -> p j")
        assert at[0] <= 33024
        pr = [sb(f"pr{n}", [P, TOPK], u32) for n in range(TG)]
        prm = h1[:, :, :].rearrange("p t d -> p (t d)")
        ldt, iA, Ai = prm[:, 126:128], prm[:, 128:256], prm[:, 256:384]
        expin = prm[:, 126:256]
        Bi = prm[:, 384:640].rearrange("p (m r) -> p m r", r=2)
        zt = xn2[:, :, :].rearrange("p t d -> p (t d)")
        zz = [zt[:, P * n:P * (n + 1)] for n in range(6)]
        wT = attn[:, 0:2, :].rearrange("p t (k h) -> p (t k) h", h=P)
        shraw = [gbuf[0][:, 0:2, :], gbuf[1][:, 0:2, :], hres[0][:, 0:2, :]]
        rwraw = hres[1][0:NE, 0, :]

        bank = [ctx.enter_context(nc.psum_tensor(f"bank{n}", [P, 512], f32)) for n in range(8)]
        BS, BP, BM = bank[0:4], bank[4:6], bank[6:8]

        s_par = sem("s_par")
        s_x = sem("s_x")
        s_const = sem("s_const")
        s_shw = sem("s_shw")
        s_ids = sem("s_ids")
        pre_dve = sem("pre_dve")
        pre_tr = sem("pre_tr")
        pre_ev = sem("pre_ev")
        cb_done = sem("cb_done")
        chunk_dve = sem("chunk_dve")
        chunk_ready = sem("chunk_ready")
        chunk_a0 = sem("chunk_a0")
        kern_full = sem("kern_full")
        kern_ev = sem("kern_ev")
        kern_st = [sem(f"kern_st{n}") for n in range(4)]
        presets = sem("presets")
        text_sp = [sem(f"text_sp{n}") for n in range(2)]
        text_pool = [sem(f"text_pool{n}") for n in range(2)]
        rows_in = [sem(f"rows_in{n}") for n in range(2)]
        g_used = sem("g_used")
        d_ln = sem("d_ln")
        d_rope = sem("d_rope")
        d_out = sem("d_out")
        xn_ready = sem("xn_ready")
        st_ready = sem("st_ready")
        m_full = sem("m_full")
        m_read = [sem(f"m_read{n}") for n in range(2)]
        a_full = sem("a_full")
        a_read = sem("a_read")
        mxt_done = sem("mxt_done")
        stat_ready = sem("stat_ready")
        b_full = sem("b_full")
        max_ready = sem("max_ready")
        exp_done = sem("exp_done")
        pv_done = sem("pv_done")
        ot_ready = sem("ot_ready")
        xn2_ready = sem("xn2_ready")
        tanh_done = sem("tanh_done")
        h2_out = sem("h2_out")
        oh_ready = sem("oh_ready")
        pos_ready = sem("pos_ready")
        x_scat = sem("x_scat")
        post_dve = sem("post_dve")
        tab_full = sem("tab_full")
        tails = sem("tails")
        w_exp = sem("w_exp")
        pw_exp = sem("pw_exp")
        x_in = [sem(f"x_in{n}") for n in range(TG)]
        t_full = [sem(f"t_full{n}") for n in range(4)]
        xT_done, th_done, hT_done = sem("xT_done"), sem("th_done"), sem("hT_done")
        sg_done, hd_done, yb_done = sem("sg_done"), sem("hd_done"), sem("yb_done")
        y_out = [sem(f"y_out{n}") for n in range(TG)]
        pr_done = sem("pr_done")
        y_in = [sem(f"y_in{n}") for n in range(TG)]
        h_in = [sem(f"h_in{n}") for n in range(TG)]
        mix1, mix2 = sem("mix1"), sem("mix2")
        passed = {eng: sem(f"passed_{n}") for eng, n in ((nc.sync, "sp"), (nc.gpsimd, "pool"), (nc.vector, "dve"))}
        out_st = [sem(f"out_st{n}") for n in range(TG)]

        def parts_value(part, b, f, o, c):
            if part == "F":
                return c if is_batch(b, 0) else val(b, f + o, c - o)
            return val(b, f + o, c + (f if is_batch(b, NB - 1) else 2 * f))

        def filled(part, b, u):
            return parts_value(part, b, len(F_READS), len(O_READS), u + 1)

        def was_read(part, b, u, n):
            return parts_value(part, b, reads(F_READS, len(F_READS), n), reads(O_READS, len(O_READS), n),
                               reads(F_READS if part == "F" else O_READS, u, n))

        def wait_filled(eng, part, b, u):
            eng.wait_ge(m_full, filled(part, b, u))

        def wait_read(eng, part, b, first, last):
            for u in range(max(first, last - 1), last + 1):
                eng.wait_ge(m_read[u % 2], was_read(part, b, u + 1, u % 2))

        def wait(eng, s, v):
            if not isinstance(v, int) or v > 0:
                eng.wait_ge(s, v)

        def pass_on(eng):
            eng.sem_inc(passed[eng], 1)

        O_AT = {0: ["norm"], 3: ["attnT"], 4: ["proj"], 8: ["xn2T"], 9: ["router", "ffn0"],
                11: ["rank", "ffn1"], 14: ["down"]}
        F_AT = {0: ["xnT"], 1: ["qkv-0"], 2: ["qkv-1"], 3: ["qkv-2", "split-0"],
                **{s: [f"split-{s - 3}"] for s in range(4, 15)}}

        def stage(name):
            kind, _, n = name.partition("-")
            return kind, int(n or 0)

        def in_pairs(batch, eng, peeled=1):
            for off in range(2 * peeled):
                batch((None, off))
            with eng.Fori(peeled, NB // 2 - 1) as i:
                for off in (0, 1):
                    batch((i, off))
            for off in (NB - 2, NB - 1):
                batch((None, off))

        def in_fours(tile, count, eng, behind=0):
            for off in range(TG):
                tile((None, off))
            with eng.Fori(1, count // TG) as i:
                for off in range(TG):
                    tile((i, off))
            for off in range(count, count + behind):
                tile((None, off))

        def earlier(t, n):
            return t[0], t[1] - n

        def index(t):
            i, off = t
            return off if i is None else i * TG + off

        def tv_(t, c):
            return val(t, 1, c, TG)

        def ring(t, c=1):
            i, off = t
            return 16 * c * (off // TG + 1) if i is None else i * (16 * c) + 16 * c * (off // TG + 1)

        def in_range(t, lo, hi):
            return t[0] is not None or lo <= t[1] < hi

        def gather(eng, b, first, count, signal):
            i, off = b
            if first in (0, SP_TOK):
                if not (is_batch(b, 0) or is_batch(b, 1)):
                    eng.wait_ge(signal[off % 2], half((i, off - 2), 16 * (SP_TOK if first == 0 else NT - SP_TOK)))
                    pass_on(eng)
            eng.wait_ge(s_ids, 16)
            with eng.Fori(0, count // TU) as j:
                at_ = [j * TU + (batch_index(b) * NT + first + n) for n in range(TU)]
                _, cols = nc.values_load_multi_w_load_instructions(ids[0:1, bass.ds(at_[0], TU)], [eng.engine], min_val=0, max_val=VOCAB - 1)
                for t, col in zip(at_, cols):
                    eng.dma_start(text_d[bass.ds(t, 1), :], txt_W[:, bass.ds(col, 1)].rearrange("h o -> o h"),
                                  allow_slow_non_contiguous=True).then_inc(signal[off % 2], 16)

        def zero_tails(eng, first):
            _, rows = nc.values_load_multi_w_load_instructions(ends[0:1, first * NE // 2:(first + 1) * NE // 2],
                                                               [eng.engine], min_val=0, max_val=NE * REG - P)
            for r in rows:
                eng.dma_start(x_d[bass.ds(r, P), :], zero).then_inc(tails, 16)

        def store_kernel(act, u):
            act.wait_ge(kern_full, u + 1)
            if u >= 4:
                act.wait_ge(kern_st[u % 4], 16 * (u // 4))
            S.copy(KS[u % 4], bank[u % 8][:, :].rearrange("p (h b) -> p h b", h=8)).then_inc(kern_ev, 1)
            act.wait_ge(kern_ev, u + 1)
            dst = kern_d[8 * u:8 * u + 8, :, :, :].rearrange("h s c (a b) -> (s c a) h b", a=LA)
            act.dma_start(dst, KS[u % 4]).then_inc(kern_st[u % 4], 16)

        def store_out(act, b):
            wait_read(act, "O", b, DOWN_USE, DOWN_USE + 1)
            dst = h2_d[bass.ds(batch_index(b), 1), :, :].rearrange("o (t p) d -> p (o t) d", p=P)
            act.dma_start(dst, h2[:]).then_inc(h2_out, 16)

        block = ctx.enter_context(nc.Block())

        @block.sync
        def _(sp):
            two = "(k p) n -> p k n"
            sp.dma_start(ldt, log_dt.rearrange("(s p) -> p s", p=P), allow_slow_non_contiguous=True).then_inc(s_par, 16)
            sp.dma_start(iA.rearrange("p (s n) -> p s n", s=2), inv_A_real.rearrange("(s p) n -> p s n", p=P)).then_inc(s_par, 16)
            sp.dma_start(Ai.rearrange("p (s n) -> p s n", s=2), A_imag.rearrange("(s p) n -> p s n", p=P)).then_inc(s_par, 16)
            sp.dma_start(prm[:, 384:640].rearrange("p (s m) -> p s m", s=2),
                         B_ri.rearrange("(s p) n r -> p s (n r)", p=P)).then_inc(s_par, 16)
            sp.dma_start(ident[:], identity).then_inc(s_const, 16)
            sp.dma_start(ids[:], x_txt.rearrange("b t -> (b t)").unsqueeze(0)).then_inc(s_ids, 16)
            for c in range(0, NB, 4):
                for s in range(2):
                    sp.dma_start(xin[:, c:c + 4, s, :],
                                 x[c:c + 4, s * P:(s + 1) * P, :, :].rearrange("c p n r -> p c (n r)")).then_inc(s_x, 16)
            for raw, src in zip(shraw, (sh_gate, sh_up, sh_down)):
                sp.dma_start(raw, src.rearrange(two, p=P)).then_inc(s_shw, 16)
            sp.dma_start(rwraw, router_w).then_inc(s_shw, 16)
            sp.dma_start(wqkv[:], w_qkv.rearrange(two, p=P)).then_inc(s_const, 16)
            sp.dma_start(wout[:], w_out.rearrange(two, p=P)).then_inc(s_const, 16)
            sp.dma_start(cos[:], rope_cos).then_inc(s_const, 16)
            sp.dma_start(sin[:], rope_sin).then_inc(s_const, 16)
            sp.dma_start(bout[:], b_out.partition_broadcast(P)).then_inc(s_const, 16)
            sp.dma_start(btxt[:], txt_b.partition_broadcast(P)).then_inc(s_const, 16)
            sp.dma_start(pfx[:], prefix).then_inc(s_const, 16)
            sp.dma_start(erow[:], expert_rows).then_inc(s_const, 16)
            sp.dma_start(rbias[:], router_bias.partition_broadcast(P)).then_inc(s_const, 16)

            def load(b):
                i, off = b
                par = off % 2
                sp.wait_ge(text_sp[par], half(b, 16 * SP_TOK))
                pass_on(sp)
                sp.wait_ge(text_pool[par], half(b, 16 * (NT - SP_TOK)))
                wait(sp, g_used, val(b, 1, -1))
                pass_on(sp)
                c = batch_index(b)
                if is_batch(b, 0):
                    for n in range(4):
                        sp.wait_ge(kern_st[n], 64)
                    sp.wait_ge(pre_tr, 3)
                sp.dma_start(gbuf[par][:, 0:2, :],
                             kern_d[:, :, bass.ds(c, 1), :].rearrange("p s o l -> p s (o l)")).then_inc(rows_in[par], 16)
                sp.dma_start(gbuf[par][:, 2, :], text_d[bass.ds(c * NT, NT), :]).then_inc(rows_in[par], 16)

            sp.wait_ge(s_ids, 16)

            def batch(b):
                gather(sp, b, 0, SP_LEAD, text_sp)
                if not is_batch(b, 0):
                    load((b[0], b[1] - 1))
                gather(sp, b, SP_LEAD, SP_TOK - SP_LEAD, text_sp)

            in_pairs(batch, sp)
            load((None, NB - 1))

            sp.wait_ge(post_dve, POST_STEPS)
            sp.wait_ge(x_scat, 16 * SLOTS * NB)
            sp.dma_start(x_d[NE * REG:XROWS, :], zero).then_inc(tails, 16)
            zero_tails(sp, 0)
            sp.wait_ge(pw_exp, 2)
            sp.wait_ge(tails, 16 * (NE + 1))

            def tile(t):
                if in_range(t, 0, NTILE):
                    if not in_range(t, 0, TG) or t[0] is not None:
                        sp.wait_ge(t_full[0], tv_(t, 1 - TG))
                    r = sp.value_load(tab[0:1, bass.ds(index(t), 1)], min_val=0, max_val=XROWS - P)
                    sp.dma_start(xb[t[1] % TG], x_d[bass.ds(r, P), :]).then_inc(x_in[t[1] % TG], 16)

            in_fours(tile, NTILE, sp)
            sp.wait_ge(h2_out, 16 * NB)

            def mix(t):
                if t[0] is not None:
                    sp.wait_ge(mix1, tv_(t, 1 - TG))
                sp.dma_start(hb[t[1] % TG], h2_d.rearrange("b t d -> (b t) d")[bass.ds(index(t) * P, P), :])\
                    .then_inc(h_in[t[1] % TG], 16)

            in_fours(mix, NB * TT, sp)
            for n in range(TG):
                sp.wait_ge(out_st[n], 16 * NB * TT // TG)

        @block.gpsimd
        def _(pool):
            pool.wait_ge(s_ids, 16)
            def scatter(b):
                pool.wait_ge(pos_ready, val(b, 1, 1))
                pass_on(pool)
                for j in range(SLOTS):
                    pool.indirect_dma_start(x_d[:, :], bass.IndirectOffsetOnAxis(ap=pos[:, j:j + 1], axis=0),
                                            xn2[:, j // TOPK, :], None).then_inc(x_scat, 16)

            def batch(b):
                gather(pool, b, SP_TOK, NT - SP_TOK, text_pool)
                if not any(is_batch(b, n) for n in range(3)):
                    scatter((b[0], b[1] - 3))

            in_pairs(batch, pool, 2)
            scatter((None, NB - 3))
            scatter((None, NB - 2))
            scatter((None, NB - 1))

            def store(t):
                pool.wait_ge(yb_done, tv_(t, 1))
                pass_on(pool)
                pool.dma_start(y_d[bass.ds(index(t) * P, P), :], yb[t[1] % TG]).then_inc(y_out[t[1] % TG], 16)

            in_fours(store, NTILE, pool)
            for n in range(TG):
                pool.wait_ge(y_out[n], 16 * NTILE // TG)

            def mix(t):
                pool.wait_ge(pr_done, tv_(t, 1))
                pass_on(pool)
                for k in range(TOPK):
                    pool.indirect_dma_start(ya[t[1] % TG][k], None, y_d[:, :],
                                            bass.IndirectOffsetOnAxis(ap=pr[t[1] % TG][:, k:k + 1], axis=0))\
                        .then_inc(y_in[t[1] % TG], 16)

            in_fours(mix, NB * TT, pool)

        @block.scalar
        def _(act):
            for n, dst in enumerate((shg_t, shu_t, shd_t)):
                act.wait_ge(pre_tr, n + 1)
                S.copy(dst[:, :, :].rearrange("p k n -> p (k n)"), bank[n][:]).then_inc(pre_ev, 1)
            act.wait_ge(pre_tr, 4)
            S.copy(rw_t[:, :, :].rearrange("p k n -> p (k n)"), bank[3][:, 0:2 * NE]).then_inc(pre_ev, 1)
            for q in range(NCH):
                act.wait_ge(cb_done, NB // 4)
                if q >= 2:
                    act.wait_ge(kern_full, 4 * (q - 1))
                for r, sign in ((0, 1.0), (1, -1.0)):
                    S.activation(CC[q % 2][r][:, :, :, 0],
                                 CB[r][:, :, q * HC:(q + 1) * HC].rearrange("p c h -> p h c"),
                                 ACT.Copy, scale=sign).then_inc(chunk_a0, 1)
                if q >= 1:
                    for u in range(4 * (q - 1), 4 * q):
                        store_kernel(act, u)
            for u in range(4 * (NCH - 1), 4 * NCH):
                store_kernel(act, u)

            def v_copy(b, t):
                par = b[1] % 2
                u = QKV_USE + 2 * t + 1
                wait_filled(act, "F", b, u)
                if t == 0:
                    wait(act, pv_done, val(b, NH, -NH))
                S.copy(VP[par][:, t, :, 0:DH], BM[1][:, 0:D].rearrange("p (h d) -> p h d", h=NH))\
                    .then_inc(m_read[1], 1)

            def f_stage(b, name):
                par = b[1] % 2
                kind, t = stage(name)
                if kind == "xnT":
                    transposed(b, "F", X_USE, xnT)
                elif kind == "qkv":
                    v_copy(b, t)
                elif kind == "split":
                    u = SPLIT_USE + t
                    cols = slice(t // 4 * P, (t // 4 + 1) * P)
                    n = t % 2
                    wait_filled(act, "F", b, u)
                    if t % 4 < 2:
                        S.copy(QT[par][:, 4 * n:4 * n + 4, cols],
                               BM[n][:, :].rearrange("p (c q) -> p c q", c=4)).then_inc(m_read[n], 1)
                    else:
                        for odd in range(2):
                            rows = slice(64 * odd, 64 * odd + 64)
                            S.copy(KT[par][rows, 8 * n + odd:8 * n + 8:2, cols],
                                   BM[n][rows, :].rearrange("p (c q) -> p c q", c=4)).then_inc(m_read[n], 1)

            def transposed(b, part, u, dst):
                for k in range(2):
                    wait_filled(act, part, b, u + k)
                    S.copy(dst[:, k, :], BM[(u + k) % 2][:, 0:T]).then_inc(m_read[(u + k) % 2], 1)

            def o_stage(b, name):
                if name == "attnT":
                    transposed(b, "O", ATT_USE, attnT)
                elif name == "xn2T":
                    act.wait_ge(stat_ready, val(b, 2, 2))
                    wait(act, x_scat, val(b, 16 * SLOTS, 0))
                    for t in range(TT):
                        S.activation(xn2[:, t, :], h1[:, t, :], ACT.Identity, scale=factor[:, t:t + 1],
                                     bias=shift[:, t:t + 1]).then_inc(xn2_ready, 1)
                    transposed(b, "O", X2_USE, xn2T)
                elif name in ("ffn0", "ffn1"):
                    u = FFN_USE[int(name[-1])]
                    wait_filled(act, "O", b, u)
                    S.activation(tg, BM[u % 2][:, 0:T], ACT.Tanh, scale=0.5).then_inc(tanh_done, 1)

            def h1_half(b, o_b):
                for s in range(NH):
                    for name in O_AT.get(s, []) if o_b else []:
                        o_stage(o_b, name)
                if o_b:
                    store_out(act, o_b)
                act.wait_ge(a_full, val(b, 49, 49))
                S.copy(mxT[:, :], BS[0][0:2 * NH, 0:T]).then_inc(mxt_done, 1)

            def h2_half(b, f_b):
                for s in range(NH):
                    for t in range(TT):
                        u = TT * s + t
                        act.wait_ge(b_full, val(b, 48, u + 1))
                        wait(act, pv_done, val(b, NH, s - 1))
                        S.activation(EX[:, u % 6, :], BS[u % 4][:, 0:T], ACT.Exp).then_inc(exp_done, 1)
                    for name in F_AT.get(s, []) if f_b else []:
                        f_stage(f_b, name)

            act.wait_ge(presets, 5)
            for name in sum(F_AT.values(), []):
                f_stage((None, 0), name)

            def batch(b):
                i, off = b
                if is_batch(b, NB - 1):
                    for n, w in enumerate((gate_proj, up_proj)):
                        for k in range(2):
                            dst = wgu[:, k, :].rearrange("p (e n m) -> p e n m", e=NE, n=2)[:, :, n, :]
                            act.dma_start(dst, w[:, k * P:(k + 1) * P, :].rearrange("e p m -> p e m")).then_inc(w_exp, 16)
                    act.dma_start(wdn.rearrange("p (e d) -> p e d", e=NE),
                                  down_proj.rearrange("e p d -> p e d")).then_inc(w_exp, 16)
                h1_half(b, None if is_batch(b, 0) else (i, off - 1))
                h2_half(b, None if is_batch(b, NB - 1) else (i, off + 1))

            in_pairs(batch, act)
            for name in sum(O_AT.values(), []):
                o_stage((None, NB - 1), name)
            store_out(act, (None, NB - 1))

            act.wait_ge(post_dve, 2)
            S.activation(pw[:, :, 1], pw[:, :, 0], ACT.Exp).then_inc(pw_exp, 1)
            act.wait_ge(post_dve, POST_STEPS)
            act.wait_ge(x_scat, 16 * SLOTS * NB)
            zero_tails(act, 1)
            act.wait_ge(tab_full, 1)
            S.copy(tab[:, :], bank[0][0:1, 0:2 * P]).then_inc(pw_exp, 1)

            def tile(t):
                n = t[1] % 2
                if in_range(t, 0, NTILE):
                    act.wait_ge(t_full[0], tv_(t, 1))
                    S.copy(xT[n].rearrange("p k t -> p (k t)"), bank[n][:, 0:D]).then_inc(xT_done, 1)
                s = earlier(t, 1)
                if in_range(s, 0, NTILE):
                    act.wait_ge(t_full[1], tv_(s, 1))
                    S.activation(th[s[1] % 2], bank[2 + s[1] % 2][:, 0:ED], ACT.Tanh, scale=0.5).then_inc(th_done, 1)
                s = earlier(t, 2)
                if in_range(s, 0, NTILE):
                    act.wait_ge(t_full[2], tv_(s, 1))
                    S.copy(hT[s[1] % 2], bank[4 + s[1] % 2][:, 0:ED]).then_inc(hT_done, 1)

            in_fours(tile, NTILE, act, 3)

            def mix(t):
                act.wait_ge(mix2, tv_(t, 1))
                dst = out.rearrange("b t d -> (b t) d")[bass.ds(index(t) * P, P), :]
                act.dma_start(dst, ob[t[1] % TG]).then_inc(out_st[t[1] % TG], 16)

            in_fours(mix, NB * TT, act)

        @block.vector
        def _(dve):
            TM0 = [t.rearrange("p h b -> p (h b)")[:, 0:P] for t in TM]
            pre = Steps(dve, pre_dve, 10**6)
            pre.start((None, 0))

            def cmul(step, re, im, ur, ui, fr, fi, tmp, neg=False):
                step.add(V.tensor_tensor(tmp[0], ur, fr, ALU.mult))
                step.add(V.tensor_tensor(tmp[1], ui, fi, ALU.mult))
                step.add(V.tensor_tensor(tmp[2], ur, fi, ALU.mult))
                step(V.tensor_tensor(tmp[3], ui, fr, ALU.mult))
                step.add(V.tensor_tensor(re, tmp[0], tmp[1], ALU.subtract))
                if neg:
                    step(V.scalar_tensor_tensor(im, tmp[2], -1.0, tmp[3], ALU.mult, ALU.subtract))
                else:
                    step(V.tensor_tensor(im, tmp[2], tmp[3], ALU.add))

            dve.wait_ge(s_par, 64)
            xe, ne_, re_, qe = (zt[:, 192 * n:192 * n + 130] for n in range(4))
            pre(V.tensor_scalar(xe, expin, -87.0, 88.0, ALU.max, ALU.min))
            pre(V.tensor_scalar(ne_, xe, LOG2E, ROUND, ALU.mult, ALU.add))
            pre(V.tensor_scalar(ne_, ne_, ROUND, None, ALU.subtract))
            pre(V.scalar_tensor_tensor(re_, ne_, -LN2_HI, xe, ALU.mult, ALU.add))
            pre(V.scalar_tensor_tensor(re_, ne_, -LN2_LO, re_, ALU.mult, ALU.add))
            pre.add(V.tensor_scalar(xe.bitcast(i32), ne_, 127.0, float(1 << 23), ALU.add, ALU.mult))
            pre(V.tensor_scalar(qe, re_, 1.0 / math.factorial(EXP_TERMS), None, ALU.mult))
            for k in range(EXP_TERMS - 1, 0, -1):
                pre(V.scalar_tensor_tensor(qe, qe, 1.0 / math.factorial(k), re_, ALU.add, ALU.mult))
            pre(V.scalar_tensor_tensor(expin, qe, 1.0, xe, ALU.add, ALU.mult))
            dt_ = ldt
            zr, zi, t0, t1, t2, t3 = zz
            for s in range(2):
                cs_ = slice(s * N, (s + 1) * N)
                pre.add(V.tensor_scalar(zr[:, cs_], iA[:, cs_], dt_[:, s:s + 1], -0.5, ALU.mult, ALU.mult))
                pre(V.tensor_scalar(zi[:, cs_], Ai[:, cs_], dt_[:, s:s + 1], 0.5, ALU.mult, ALU.mult))
            pre.add(V.tensor_tensor(t0, zr, zr, ALU.mult))
            pre.add(V.tensor_tensor(t1, zi, zi, ALU.mult))
            pre(V.tensor_scalar(t2, zr, -1.0, 1.0, ALU.mult, ALU.add))
            pre.add(V.tensor_tensor(t2, t2, t2, ALU.mult))
            pre(V.tensor_tensor(t3, t0, t1, ALU.add))
            pre(V.tensor_tensor(t2, t2, t1, ALU.add))
            pre.add(V.tensor_scalar(t3, t3, -1.0, 1.0, ALU.mult, ALU.add))
            pre(V.reciprocal(t2, t2))
            pre.add(V.tensor_tensor(t0, t3, t2, ALU.mult))
            pre(V.scalar_tensor_tensor(t1, zi, 2.0, t2, ALU.mult, ALU.mult))
            pre.add(V.tensor_scalar(zr, Bi[:, :, 0], 2.0, None, ALU.mult))
            pre(V.tensor_scalar(zi, Bi[:, :, 1], 2.0, None, ALU.mult))
            n_par = pre.k
            assert n_par == PAR_STEPS, n_par
            dve.wait_ge(pre_tr, 5)
            pre(V.tensor_copy(wT, bank[4][:, :].rearrange("p (k h) -> p k h", h=P)))
            assert pre.k == WT_STEP
            pre.add(V.tensor_copy(PW[:, 0, :, :], wT[:, 0:2, :]))
            pre.done()
            for k in range(7):
                a, c = PW[:, k, 0, :], PW[:, k, 1, :]
                pre.add(V.tensor_tensor(TM0[0], a, a, ALU.mult))
                pre.add(V.tensor_tensor(TM0[1], c, c, ALU.mult))
                pre(V.scalar_tensor_tensor(PW[:, k + 1, 1, :], a, 2.0, c, ALU.mult, ALU.mult))
                pre(V.tensor_tensor(PW[:, k + 1, 0, :], TM0[0], TM0[1], ALU.subtract))
            cmul(pre, PW[:, 8, 0, :], PW[:, 8, 1, :], PW[:, 6, 0, :], PW[:, 6, 1, :],
                 PW[:, 7, 0, :], PW[:, 7, 1, :], TM0)
            for g in range(NB // 4):
                dve.wait_ge(pre_tr, 6 + g)
                pair = (4, 5) if g % 2 == 0 else (6, 7)
                ur, ui = (bank[n][:, :].rearrange("p (c h) -> p c h", c=4) for n in pair)
                br, bi = (wT[:, 2 + r, :].unsqueeze(1).to_broadcast([P, 4, P]) for r in range(2))
                tmp = [t.rearrange("p h b -> p (h b)")[:, 0:512].rearrange("p (c h) -> p c h", c=4) for t in TM]
                cmul(pre, CB[0][:, 4 * g:4 * g + 4, :], CB[1][:, 4 * g:4 * g + 4, :], ur, ui, br, bi, tmp)
                dve.sem_inc(cb_done, 1)

            ck = Steps(dve, chunk_dve, 10**6)
            ck.start((None, 0))
            for q in range(NCH):
                hp = slice(q * HC, (q + 1) * HC)
                vr, vi = VV[q % 2]
                cr, ci = CC[q % 2]
                if q >= 2:
                    dve.wait_ge(kern_full, 4 * (q - 1))
                ck.add(V.memset(vr[:, :, 0:1], 1.0))
                ck.add(V.memset(vi[:, :, 0:1], 0.0))
                ck.add(V.tensor_copy(vr[:, :, 1], PW[:, 0, 0, hp]))
                ck(V.tensor_copy(vi[:, :, 1], PW[:, 0, 1, hp]))
                for k in range(1, 6):
                    w = 1 << k
                    fr, fi = (PW[:, k, r, hp].unsqueeze(2).to_broadcast([P, HC, w]) for r in range(2))
                    tmp = [t[:, :, 0:w] for t in TM]
                    cmul(ck, vr[:, :, w:2 * w], vi[:, :, w:2 * w], vr[:, :, 0:w], vi[:, :, 0:w], fr, fi, tmp)
                br, bi = (CB[r][:, :, hp].rearrange("p c h -> p h c") for r in range(2))
                for a in range(1, LA):
                    fr, fi = (PW[:, 5 + a, r, hp].unsqueeze(2).to_broadcast([P, HC, NB]) for r in range(2))
                    tmp = [t[:, :, 0:NB] for t in TM]
                    cmul(ck, cr[:, :, :, a], ci[:, :, :, a], br, bi, fr, fi, tmp, neg=True)
                dve.sem_inc(chunk_ready, 1)

            dve.wait_ge(kern_ev, 16)
            for n in range(4):
                dve.wait_ge(kern_st[n], 64)
            dve.wait_ge(s_const, 16 * 10)
            ps = Steps(dve, presets, 10**6)
            ps.start((None, 0))
            for n in range(2):
                V.memset(KT[n][:, :, :].bitcast(f32), 0.0).then_inc(chunk_dve, 1)
            V.memset(st[:, :, :, :, MROW:QW].rearrange("p t s h w -> p (t s h) w"), 0.0).then_inc(chunk_dve, 1)
            for n in range(2):
                V.memset(VP[n][:, :, :, DH:32].rearrange("p t h w -> p (t h) w"), 0.0).then_inc(chunk_dve, 1)
            dve.wait_ge(chunk_dve, ck.k + 5)
            V.tensor_copy(pick[:, :], ident[0:2 * NH, 0:NH]).then_inc(presets, 1)
            for n in range(2):
                V.memset(VP[n][:, :, :, DH], 1.0).then_inc(presets, 1)
            V.memset(mx[:, :, :, :], 0.0).then_inc(presets, 1)
            V.tensor_copy(cum[:, 0, :], erow[:, 1, :]).then_inc(presets, 1)
            dve.wait_ge(presets, 5)

            ln = Steps(dve, d_ln, LN_STEPS)
            ro = Steps(dve, d_rope, TT * 3)
            ou = Steps(dve, d_out, OUT_STEPS)

            def layernorm(step, src, dst=None, ready=None):
                for t in range(TT):
                    step.add(V.bn_stats(bst[:, t, :], src[:, t, :]))
                step.done()
                step.add(V.memset(nwt[:, :, :], 0.0))
                for t in range(TT):
                    step.add(V.bn_aggr(mv[:, t, :], bst[:, t, :]))
                step.done()
                v, y, hv, t_ = (nwt[:, n, :] for n in range(4))
                step(V.tensor_scalar(v, mv[:, :, 1], EPS, None, ALU.add))
                step.add(V.tensor_scalar(hv, v, -0.5, None, ALU.mult))
                step(V.tensor_scalar(t_.bitcast(i32), v.bitcast(i32), 1, None, ALU.logical_shift_right))
                step(V.tensor_scalar(y.bitcast(i32), t_.bitcast(i32), -1.0, MAGIC, ALU.mult, ALU.add))
                for _ in range(3):
                    step(V.tensor_tensor(t_, y, y, ALU.mult))
                    step(V.tensor_tensor(t_, t_, hv, ALU.mult))
                    step(V.scalar_tensor_tensor(y, t_, 1.5, y, ALU.add, ALU.mult))
                if dst is None:
                    V.scalar_tensor_tensor(shift[:], mv[:, :, 0], -1.0, y, ALU.mult, ALU.mult).then_inc(stat_ready, 1)
                    V.tensor_copy(factor[:], y).then_inc(stat_ready, 1)
                    return
                for t in range(TT):
                    V.tensor_scalar(dst[:, t, :], src[:, t, :], mv[:, t, 0:1], y[:, t:t + 1],
                                    ALU.subtract, ALU.mult).then_inc(ready, 1)

            def rope(b, t):
                par = b[1] % 2
                if t == 0:
                    ro.start(b)
                u = QKV_USE + 2 * t
                wait_filled(dve, "F", b, u)
                qk = BM[0][:, :].rearrange("p (s h d) -> p s h d", s=2, h=NH)
                sh = [P, 2, NH, DH]
                a4, b4, c4 = (r[:, :, :].rearrange("p (s h) d -> p s h d", s=2) for r in (ra, rb, rc))
                cs = cos[:, t, :, :].unsqueeze(2).to_broadcast(sh)
                sn = sin[:, t, :, :].unsqueeze(2).to_broadcast(sh)
                V.tensor_tensor(a4, qk, cs, ALU.mult).then_inc(m_read[0], 1)
                hd = DH // 2
                for f in range(2):
                    o = slice(f * hd, f * hd + hd)
                    i_ = slice((1 - f) * hd, (1 - f) * hd + hd)
                    V.tensor_tensor(b4[:, :, :, o], qk[:, :, :, i_], sn[:, :, :, o], ALU.mult).then_inc(m_read[0], 1)
                wait_read(dve, "F", b, u, u)
                ro(V.tensor_tensor(rc[:, :, :], ra[:, :, :], rb[:, :, :], ALU.add))
                q_, k_ = st[:, t, 0, :, :], st[:, t, 1, :, :]
                for s, dst, step in ((0, q_, 2), (1, k_, 1)):
                    rep = dst[:, :, 0:MROW].rearrange("p h (n d) -> p h n d", d=DH)[:, :, 0:3:step, :] if step == 2 \
                        else dst[:, :, 0:2 * DH].rearrange("p h (n d) -> p h n d", d=DH)
                    src = rc[:, NH * s:NH * (s + 1), :].unsqueeze(2).to_broadcast([P, NH, 2, DH])
                    ro.add(V.tensor_scalar(rep.bitcast(i32), src.bitcast(i32), SPLIT, None, ALU.bitwise_and))
                ro.done()
                V.tensor_tensor(q_[:, :, DH:2 * DH], rc[:, 0:NH, :], q_[:, :, 0:DH], ALU.subtract)\
                    .then_inc(st_ready, 1)
                V.tensor_tensor(k_[:, :, 2 * DH:3 * DH], rc[:, NH:2 * NH, :], k_[:, :, 0:DH], ALU.subtract)\
                    .then_inc(st_ready, 1)
                dve.wait_ge(st_ready, val(b, 2 * TT, 2 * t + 2))
                if t == TT - 1:
                    ro.end()

            def f_stage(b, name):
                par = b[1] % 2
                kind, t = stage(name)
                if kind == "rows":
                    ln.start(b)
                    g = gbuf[par]
                    dve.wait_ge(rows_in[par], half(b, 32))
                    ln(V.tensor_tensor(g[:, 2, :], g[:, 2, :], btxt[:], ALU.add))
                    layernorm(ln, g, xn, xn_ready)
                    ln.end()
                elif kind == "xnT":
                    V.tensor_tensor(hres[par][:], gbuf[par][:], bout[:].unsqueeze(1).to_broadcast([P, TT, D]), ALU.add)\
                        .then_inc(g_used, 1)
                elif kind == "qkv":
                    rope(b, t)

            def o_stage(b, name):
                par = b[1] % 2
                if name == "norm":
                    ou.start(b)
                    for t in range(TT):
                        u = NORM_USE + t
                        wait_filled(dve, "O", b, u)
                        o4 = BM[u % 2][:, :].rearrange("p (h w) -> p h w", h=NH)
                        ou(V.reciprocal(rs[:, t, :], o4[:, :, DH]))
                        V.tensor_tensor(attn[:, t, :].rearrange("p (h d) -> p h d", h=NH), o4[:, :, 0:DH],
                                        rs[:, t, :].unsqueeze(2).to_broadcast([P, NH, DH]), ALU.mult)\
                            .then_inc(m_read[u % 2], 1)
                elif name == "proj":
                    for t in range(TT):
                        u = PROJ_USE + t
                        wait_filled(dve, "O", b, u)
                        V.tensor_tensor(h1[:, t, :], BM[u % 2][:, 0:D], hres[par][:, t, :], ALU.add)\
                            .then_inc(m_read[u % 2], 1)
                    wait_read(dve, "O", b, PROJ_USE, PROJ_USE + 2)
                    layernorm(ou, h1)
                elif name == "router":
                    u = ROUTE_USE
                    wait_filled(dve, "O", b, u)
                    V.tensor_tensor(lg[:], BM[u % 2][:, 0:TT * NE].rearrange("p (t e) -> p t e", t=TT),
                                    rbias[:].unsqueeze(1).to_broadcast([P, TT, NE]), ALU.add)\
                        .then_inc(m_read[u % 2], 1)
                    wait_read(dve, "O", b, u, u)
                    pass_on(dve)
                    c = batch_index(b) * TT
                    for t in range(TT):
                        ou.add(V.max(tv[:, t, :], lg[:, t, :]))
                    ou.done()
                    pass_on(dve)
                    for t in range(TT):
                        ou.add(V.max_index(ti[:, t, :], tv[:, t, :], lg[:, t, :]))
                    ou.done()
                    ou.add(V.tensor_copy(topv[:, bass.ds(c, TT), :], tv[:, :, 0:TOPK]))
                    ou(V.tensor_copy(ef[:, :].rearrange("p (t k) -> p t k", k=TOPK), ti[:, :, 0:TOPK]))
                    sh = [P, SLOTS, NE]
                    V.tensor_tensor(oh[:], erow[:, 0:1, :].to_broadcast(sh), ef[:, :].unsqueeze(2).to_broadcast(sh),
                                    ALU.is_equal).then_inc(oh_ready, 1)
                elif name == "rank":
                    u = RANK_USE
                    ps = BM[u % 2][:, 0:2 * SLOTS * NE].rearrange("p (n j e) -> p n j e", n=2, j=SLOTS)
                    wait_filled(dve, "O", b, u)
                    r0 = was_read("O", b, u, u % 2)
                    for j in range(SLOTS):
                        V.tensor_tensor(cum[:, j + 1, :], cum[:, j, :], ps[:, 1, j, :], ALU.add)\
                            .then_inc(m_read[u % 2], 1)
                        dve.wait_ge(m_read[u % 2], r0 + (j + 1))
                    V.tensor_tensor(rk[:], ps[:, 0, :, :], cum[:, 0:SLOTS, :], ALU.add).then_inc(m_read[u % 2], 1)
                    wait_read(dve, "O", b, u, u)
                    ou(V.tensor_tensor(rk[:], rk[:], oh[:], ALU.mult))
                    ou(V.tensor_reduce(posf[:], rk[:], AX.X, ALU.add))
                    ou.add(V.tensor_copy(cum[:, 0, :], cum[:, SLOTS, :]))
                    ou.add(V.tensor_copy(pos_all[:, bass.ds(batch_index(b) * SLOTS, SLOTS)], posf[:]))
                    ou.add(V.tensor_copy(ef_all[:, bass.ds(batch_index(b) * SLOTS, SLOTS)], ef[:]))
                    V.tensor_copy(pos[:], posf[:]).then_inc(pos_ready, 1)
                    dve.wait_ge(pos_ready, val(b, 1, 1))
                    ou.done()
                    ou.end()
                elif name in ("ffn0", "ffn1"):
                    e = int(name[-1])
                    u = FFN_USE[e]
                    dve.wait_ge(tanh_done, val(b, 2, e + 1))
                    V.scalar_tensor_tensor(tu, tg, 1.0, BM[u % 2][:, 0:T], ALU.add, ALU.mult)\
                        .then_inc(m_read[u % 2], 1)
                    wait_read(dve, "O", b, u, u)
                    wait_filled(dve, "O", b, u + 1)
                    V.scalar_tensor_tensor(hid[:, e, :], tu, 0.5, BM[(u + 1) % 2][:, 0:T], ALU.mult, ALU.mult)\
                        .then_inc(m_read[(u + 1) % 2], 1)
                    wait_read(dve, "O", b, u + 1, u + 1)
                elif name == "down":
                    wait(dve, h2_out, val(b, 16, 0))
                    for n, tiles in enumerate(((0, 2), (2, 3))):
                        u = DOWN_USE + n
                        wait_filled(dve, "O", b, u)
                        lo, hi = tiles
                        V.tensor_tensor(h2[:, lo:hi, :],
                                        BM[u % 2][:, 0:(hi - lo) * D].rearrange("p (t d) -> p t d", d=D),
                                        h1[:, lo:hi, :], ALU.add).then_inc(m_read[u % 2], 1)

            def h1_half(b, o_b):
                wait(dve, mxt_done, val(b, 1, 0))
                for s in range(NH):
                    for t in range(TT):
                        u = TT * s + t
                        dve.wait_ge(a_full, val(b, 49, u + 1))
                        V.tensor_reduce(mx[:, t, 1, s:s + 1], BS[u % 4][:, 0:T], AX.X, ALU.max)\
                            .then_inc(a_read, 1)
                    for name in O_AT.get(s, []) if o_b else []:
                        o_stage(o_b, name)
                dve.wait_ge(a_read, val(b, 49, 48))
                V.tensor_scalar(mx[:, :, 1, :], mx[:, :, 1, :], -1.0, None, ALU.mult).then_inc(a_read, 1)
                dve.wait_ge(a_read, val(b, 49, 49))
                V.tensor_scalar(mx[:, :, 0, :].bitcast(i32), mx[:, :, 1, :].bitcast(i32), SPLIT, None,
                                ALU.bitwise_and).then_inc(max_ready, 1)
                dve.wait_ge(max_ready, val(b, 2, 1))
                V.tensor_tensor(mx[:, :, 1, :], mx[:, :, 1, :], mx[:, :, 0, :], ALU.subtract).then_inc(max_ready, 1)

            def h2_half(b, f_b, rows_b):
                for s in range(NH):
                    for name in F_AT.get(s, []) if f_b else []:
                        f_stage(f_b, name)
                    if s % 4 == 1 and s > 1:
                        ot_copy(b, s // 4 - 1)
                    if s == ROWS_AT and rows_b:
                        f_stage(rows_b, "rows")
                ot_copy(b, 3)

            def ot_copy(b, g):
                dve.wait_ge(pv_done, val(b, NH, 4 * g + 4))
                V.tensor_copy(OT[:, g, :], BP[g % 2][:, 0:T]).then_inc(ot_ready, 1)

            for name in ["rows"] + sum(F_AT.values(), []):
                f_stage((None, 0), name)
            f_stage((None, 1), "rows")

            def batch(b):
                i, off = b
                h1_half(b, None if is_batch(b, 0) else (i, off - 1))
                h2_half(b, None if is_batch(b, NB - 1) else (i, off + 1),
                        None if is_batch(b, NB - 2) or is_batch(b, NB - 1) else (i, off + 2))

            in_pairs(batch, dve)
            for name in sum(O_AT.values(), []):
                o_stage((None, NB - 1), name)

            po = Steps(dve, post_dve, 10**6)
            po.start((None, 0))
            po.add(V.memset(zero, 0.0))
            po(V.tensor_tensor(pw[:, :, 0], topv[:, :, 1], topv[:, :, 0], ALU.subtract))
            f = [rk[:, n, :] for n in range(SLOTS)]
            g = [oh[:, n, :] for n in range(SLOTS)]
            one = [posf[:, n:n + 1] for n in range(SLOTS)]
            last, tiles_, tend, tbeg, first = cum[:, 0, :], f[0], f[1], f[2], f[3]
            po.add(V.tensor_copy(ends[:], last))
            po.add(V.tensor_copy(ef[:, 0:1], erow[:, 2, 0:1]))
            po(V.tensor_tensor(f[4], last, erow[:, 1, :], ALU.subtract))
            it = lg[:, 0, :].bitcast(i32)
            po(V.tensor_scalar(it, f[4], float(P - 1), None, ALU.add))
            po(V.tensor_scalar(it, it, P.bit_length() - 1, None, ALU.logical_shift_right))
            po(V.tensor_copy(tiles_, it))
            po(V.tensor_tensor_scan(tend, erow[:, 3, :], tiles_, 0.0, ALU.mult, ALU.add))
            po(V.tensor_tensor(tbeg, tend, tiles_, ALU.subtract))
            t_ = ef[:, 0:1]
            po.add(V.tensor_scalar(g[0], tbeg, t_, None, ALU.is_le))
            po.add(V.tensor_scalar(g[1], tend, t_, None, ALU.is_le))
            po(V.scalar_tensor_tensor(first, tbeg, -float(P), erow[:, 1, :], ALU.mult, ALU.add))
            po(V.tensor_tensor(g[2], g[0], g[1], ALU.subtract))
            po.add(V.tensor_tensor(g[3], g[2], first, ALU.mult))
            po.add(V.tensor_tensor(g[4], g[2], erow[:, 0, :], ALU.mult))
            po(V.tensor_reduce(one[0], g[2], AX.X, ALU.add))
            po.add(V.tensor_reduce(one[1], g[3], AX.X, ALU.add))
            po.add(V.tensor_reduce(tabc[:, 1:2], g[4], AX.X, ALU.add))
            po.add(V.tensor_scalar(one[2], one[0], t_, float(P), ALU.mult, ALU.mult))
            po(V.tensor_scalar(one[3], one[0], -1.0, 1.0, ALU.mult, ALU.add))
            po(V.tensor_tensor(one[1], one[1], one[2], ALU.add))
            po.add(V.scalar_tensor_tensor(tabc[:, 0:1], one[3], float(NE * REG), one[1], ALU.mult, ALU.add))
            po.done()
            assert po.k == POST_STEPS, po.k
            shp = [P, NB * SLOTS, NE]
            po(V.tensor_tensor(ohall, erow[:, 0:1, :].to_broadcast(shp), ef_all[:].unsqueeze(2).to_broadcast(shp), ALU.is_equal))
            po(V.tensor_tensor(ohall, ohall, first.unsqueeze(1).to_broadcast(shp), ALU.mult))
            po(V.tensor_reduce(ef_all[:], ohall, AX.X, ALU.add))
            po(V.tensor_tensor(posy.bitcast(u32), pos_all[:], ef_all[:], ALU.subtract))
            dve.wait_ge(pw_exp, 1)
            po(V.tensor_scalar(pw[:, :, 0], pw[:, :, 1], 1.0, None, ALU.add))
            po(V.reciprocal(pw[:, :, 0], pw[:, :, 0]))
            po(V.tensor_tensor(pw[:, :, 1], pw[:, :, 1], pw[:, :, 0], ALU.mult))

            def tile(t):
                s = earlier(t, 1)
                n = s[1] % 2
                if in_range(s, 0, NTILE):
                    dve.wait_ge(th_done, tv_(s, 1))
                    gate, up = bank[2 + n][:, 0:ED], bank[2 + n][:, ED:2 * ED]
                    V.scalar_tensor_tensor(sg[n], th[n], 1.0, gate, ALU.add, ALU.mult).then_inc(sg_done, 1)
                    dve.wait_ge(sg_done, tv_(s, 1))
                    V.scalar_tensor_tensor(hd[n], sg[n], 0.5, up, ALU.mult, ALU.mult).then_inc(hd_done, 1)
                s = earlier(t, 3)
                n = s[1] % 2
                if in_range(s, 0, NTILE):
                    dve.wait_ge(t_full[3], tv_(s, 1))
                    if not in_range(s, 0, TG) or s[0] is not None:
                        dve.wait_ge(y_out[s[1] % TG], ring(earlier(s, TG)))
                    V.tensor_copy(yb[s[1] % TG], bank[6 + n][:, 0:D]).then_inc(yb_done, 1)

            in_fours(tile, NTILE, dve, 3)

            def rows(t):
                V.tensor_copy(pr[t[1] % TG][:], posy.bitcast(u32)[:, bass.ds(index(t) * TOPK, TOPK)]).then_inc(pr_done, 1)

            def mix(t):
                n, c = t[1] % TG, index(t)
                dve.wait_ge(h_in[n], ring(t))
                dve.wait_ge(y_in[n], ring(t, TOPK))
                V.scalar_tensor_tensor(hb2[n], ya[n][0], pw[:, bass.ds(c, 1), 0], hb[n], ALU.mult, ALU.add)\
                    .then_inc(mix1, 1)
                dve.wait_ge(mix1, tv_(t, 1))
                if t[0] is not None or t[1] >= TG:
                    dve.wait_ge(out_st[n], ring(earlier(t, TG)))
                V.scalar_tensor_tensor(ob[n], ya[n][1], pw[:, bass.ds(c, 1), 1], hb2[n], ALU.mult, ALU.add)\
                    .then_inc(mix2, 1)

            def turn(t):
                s = earlier(t, TG - 1)
                if t[0] is not None or t[1] >= TG:
                    dve.wait_ge(mix2, tv_(t, 1 - TG))
                if in_range(t, 0, NB * TT):
                    rows(t)
                if in_range(s, 0, NB * TT):
                    mix(s)

            in_fours(turn, NB * TT, dve, TG - 1)

        @block.tensor
        def _(pe):
            pe.wait_ge(s_shw, 64)
            pe.wait_ge(s_const, 16 * 10)
            for n in range(3):
                for o in range(2):
                    for k in range(2):
                        ins = PE.transpose(bank[n][:, k * D + o * P:k * D + (o + 1) * P],
                                           shraw[n][:, o, k * P:(k + 1) * P], ident[:])
                ins.then_inc(pre_tr, 1)
            for k in range(2):
                ins = PE.transpose(bank[3][:, k * NE:(k + 1) * NE], rwraw[:, k * P:(k + 1) * P], ident[0:NE, 0:NE])
            ins.then_inc(pre_tr, 1)
            pe.wait_ge(pre_dve, PAR_STEPS)
            for n, src in enumerate((zz[2], zz[3], zz[0], zz[1])):
                ins = PE.transpose(bank[4][:, n * P:(n + 1) * P], src, ident[:])
            ins.then_inc(pre_tr, 1)
            pe.wait_ge(s_x, 16 * 8)
            for g in range(NB // 4):
                pair = (4, 5) if g % 2 == 0 else (6, 7)
                if g == 0:
                    pe.wait_ge(pre_dve, WT_STEP)
                if g >= 2:
                    pe.wait_ge(cb_done, g - 1)
                for c in range(4):
                    for r in range(2):
                        src = xin[:, 4 * g + c, :, :].rearrange("p s (n r) -> p (s n) r", r=2)[:, :, r]
                        ins = PE.transpose(bank[pair[r]][:, c * P:(c + 1) * P], src, ident[:])
                ins.then_inc(pre_tr, 1)
            for u in range(16):
                q = u // 4
                if u % 4 == 0:
                    pe.wait_ge(chunk_ready, q + 1)
                    pe.wait_ge(chunk_a0, 2 * (q + 1))
                if u == 0:
                    pe.wait_ge(pre_ev, 4)
                if u == 4:
                    pe.wait_ge(cb_done, 4)
                if u >= 8:
                    pe.wait_ge(kern_ev, u - 7)
                for n in range(8):
                    hp = (u % 4) * 8 + n
                    for s in range(2):
                        rows = slice(64 * s, 64 * s + 64)
                        for r in range(2):
                            ins = PE.matmul(bank[u % 8][rows, n * LB:(n + 1) * LB],
                                            CC[q % 2][r][rows, hp, :, :].rearrange("p c a -> p (c a)"),
                                            VV[q % 2][r][rows, hp, :], start=(r == 0), stop=(r == 1),
                                            tile_position=(64 * s, 64 * s))
                ins.then_inc(kern_full, 1)

            def m_bank(part, b, u):
                wait(pe, m_read[u % 2], was_read(part, b, u, u % 2))
                return BM[u % 2]

            def rows_transposed(part, b, u, src):
                for k in range(2):
                    ps = m_bank(part, b, u + k)
                    for n in range(TT):
                        ins = PE.transpose(ps[:, n * P:(n + 1) * P], src[:, n, k * P:(k + 1) * P], ident[:])
                    ins.then_inc(m_full, 1)

            def f_stage(b, name):
                par = b[1] % 2
                kind, t = stage(name)
                if kind == "xnT":
                    pe.wait_ge(xn_ready, val(b, TT, TT))
                    rows_transposed("F", b, X_USE, xn)
                elif kind == "qkv":
                    wait_read(pe, "F", b, X_USE, X_USE + 1)
                    for part, (lo, hi) in enumerate(((0, 2 * D), (2 * D, 3 * D))):
                        ps = m_bank("F", b, QKV_USE + 2 * t + part)
                        for k in range(2):
                            ins = PE.matmul(ps[:, 0:hi - lo], xnT[:, k, t * P:(t + 1) * P], wqkv[:, k, lo:hi],
                                            start=(k == 0), stop=(k == 1))
                        ins.then_inc(m_full, 1)
                elif kind == "split":
                    tile, s, n = t // 4, t // 2 % 2, t % 2
                    pe.wait_ge(st_ready, val(b, 2 * TT, 2 * tile + 2))
                    ps = m_bank("F", b, SPLIT_USE + t)
                    for c in range(4):
                        src = st[:, tile, s, 8 * n + 2 * c:8 * n + 2 * c + 2, :].rearrange("p h w -> p (h w)")
                        ins = PE.transpose(ps[:, c * P:(c + 1) * P], src, ident[:])
                    ins.then_inc(m_full, 1)

            def o_stage(b, name):
                if name == "norm":
                    pe.wait_ge(ot_ready, val(b, 4, 4))
                    for t in range(TT):
                        ps = m_bank("O", b, NORM_USE + t)
                        for g in range(4):
                            ins = PE.transpose(ps[:, g * P:(g + 1) * P], OT[:, g, t * P:(t + 1) * P], ident[:])
                        ins.then_inc(m_full, 1)
                elif name == "attnT":
                    wait_read(pe, "O", b, NORM_USE, NORM_USE + 2)
                    rows_transposed("O", b, ATT_USE, attn)
                elif name == "proj":
                    wait_read(pe, "O", b, ATT_USE, ATT_USE + 1)
                    for t in range(TT):
                        ps = m_bank("O", b, PROJ_USE + t)
                        for k in range(2):
                            ins = PE.matmul(ps[:, 0:D], attnT[:, k, t * P:(t + 1) * P], wout[:, k, :],
                                            start=(k == 0), stop=(k == 1))
                        ins.then_inc(m_full, 1)
                elif name == "xn2T":
                    pe.wait_ge(xn2_ready, val(b, TT, TT))
                    rows_transposed("O", b, X2_USE, xn2)
                elif name == "router":
                    wait_read(pe, "O", b, X2_USE, X2_USE + 1)
                    ps = m_bank("O", b, ROUTE_USE)
                    for t in range(TT):
                        for k in range(2):
                            ins = PE.matmul(ps[:, t * NE:(t + 1) * NE], xn2T[:, k, t * P:(t + 1) * P], rw_t[:, k, :],
                                            start=(k == 0), stop=(k == 1))
                    ins.then_inc(m_full, 1)
                elif name == "rank":
                    pe.wait_ge(oh_ready, val(b, 1, 1))
                    ps = m_bank("O", b, RANK_USE)
                    for n in range(2):
                        ins = PE.matmul(ps[:, n * SLOTS * NE:(n + 1) * SLOTS * NE], pfx[:, n, :],
                                        oh[:, :, :].rearrange("p j e -> p (j e)"), start=True, stop=True)
                    ins.then_inc(m_full, 1)
                elif name in ("ffn0", "ffn1"):
                    e = int(name[-1])
                    for n, w in enumerate((shg_t, shu_t)):
                        ps = m_bank("O", b, FFN_USE[e] + n)
                        for k in range(2):
                            ins = PE.matmul(ps[:, 0:T], w[:, k, e * P:(e + 1) * P], xn2T[:, k, :],
                                            start=(k == 0), stop=(k == 1))
                        ins.then_inc(m_full, 1)
                elif name == "down":
                    wait_read(pe, "O", b, FFN_USE[0] + 1, FFN_USE[1] + 1)
                    for t in range(TT):
                        if t != 1:
                            ps = m_bank("O", b, DOWN_USE + t // 2)
                        for k in range(2):
                            ins = PE.matmul(ps[:, (t % 2) * D:(t % 2 + 1) * D], hid[:, k, t * P:(t + 1) * P],
                                            shd_t[:, k, :], start=(k == 0), stop=(k == 1))
                        if t:
                            ins.then_inc(m_full, 1)

            def h1_half(b, o_b):
                par = b[1] % 2
                wait_read(pe, "F", b, SPLIT_USE, len(F_READS) - 1)
                for s in range(NH):
                    for t in range(TT):
                        u = TT * s + t
                        if u < 4:
                            wait(pe, exp_done, val(b, 48, u - 3))
                        else:
                            pe.wait_ge(a_read, val(b, 49, u - 3))
                        PE.matmul(BS[u % 4][:, 0:T], QT[par][:, s // 2, t * P:(t + 1) * P],
                                  KT[par][:, s, :], start=True, stop=True).then_inc(a_full, 1)
                    for name in O_AT.get(s, []) if o_b else []:
                        o_stage(o_b, name)
                pe.wait_ge(max_ready, val(b, 2, 2))
                for t in range(TT):
                    ins = PE.transpose(BS[0][0:2 * NH, t * P:(t + 1) * P],
                                       mx[:, t, :, :].rearrange("p n h -> p (n h)"), ident[:])
                ins.then_inc(a_full, 1)

            def h2_half(b, f_b):
                par = b[1] % 2

                def pv(h, t):
                    g, j = h // 4, h % 4
                    if j == 0 and t == 0:
                        wait(pe, ot_ready, val(b, 4, g - 1))
                    pe.wait_ge(exp_done, val(b, 48, TT * h + t + 1))
                    ins = PE.matmul(BP[g % 2][32 * j:32 * j + 32, 0:T], VP[par][:, t, h, :],
                                    EX[:, (TT * h + t) % 6, :], start=(t == 0), stop=(t == TT - 1),
                                    tile_position=(0, 32 * j))
                    if t == TT - 1:
                        ins.then_inc(pv_done, 1)

                pe.wait_ge(mxt_done, val(b, 1, 1))
                for s in range(NH):
                    for t in range(TT):
                        u = TT * s + t
                        if u >= 4:
                            pe.wait_ge(exp_done, val(b, 48, u - 3))
                        PE.matmul(BS[u % 4][:, 0:T], KT[par][:, s, t * P:(t + 1) * P],
                                  QT[par][:, s // 2, :], start=True, stop=False)
                        PE.matmul(BS[u % 4][:, 0:T], pick[:, s:s + 1].to_broadcast([2 * NH, P]), mxT[:, :],
                                  start=False, stop=True).then_inc(b_full, 1)
                        if s:
                            pv(s - 1, t)
                    for name in F_AT.get(s, []) if f_b else []:
                        f_stage(f_b, name)
                for t in range(TT):
                    pv(NH - 1, t)

            for name in sum(F_AT.values(), []):
                f_stage((None, 0), name)

            def batch(b):
                i, off = b
                h1_half(b, None if is_batch(b, 0) else (i, off - 1))
                h2_half(b, None if is_batch(b, NB - 1) else (i, off + 1))

            in_pairs(batch, pe)
            for name in sum(O_AT.values(), []):
                o_stage((None, NB - 1), name)

            pe.wait_ge(post_dve, POST_STEPS)
            for n in range(2):
                ins = PE.transpose(bank[0][0:1, n * P:(n + 1) * P], tabc[:, n:n + 1], ident[:])
            ins.then_inc(tab_full, 1)
            pe.wait_ge(w_exp, 16 * 5)
            pe.wait_ge(pw_exp, 2)

            def tile(t):
                n = t[1] % 2
                if in_range(t, 0, NTILE):
                    pe.wait_ge(x_in[t[1] % TG], ring(t))
                    if t[0] is not None or t[1] >= 2:
                        pe.wait_ge(xT_done, tv_(t, -1))
                    for k in range(2):
                        ins = PE.transpose(bank[n][:, k * P:(k + 1) * P], xb[t[1] % TG][:, k * P:(k + 1) * P], ident[:])
                    ins.then_inc(t_full[0], 1)
                s = earlier(t, 1)
                n = s[1] % 2
                if in_range(s, 0, NTILE):
                    e = pe.value_load(tab[0:1, bass.ds(index(s) + P, 1)], min_val=0, max_val=NE - 1)
                    pe.wait_ge(xT_done, tv_(s, 1))
                    if s[0] is not None or s[1] >= 2:
                        pe.wait_ge(hd_done, tv_(s, -1))
                    for k in range(2):
                        ins = PE.matmul(bank[2 + n][:, 0:2 * ED], xT[n][:, k, :],
                                        wgu[:, k, bass.ds(e * (2 * ED), 2 * ED)], start=(k == 0), stop=(k == 1))
                    ins.then_inc(t_full[1], 1)
                s = earlier(t, 2)
                n = s[1] % 2
                if in_range(s, 0, NTILE):
                    pe.wait_ge(hd_done, tv_(s, 1))
                    if s[0] is not None or s[1] >= 2:
                        pe.wait_ge(hT_done, tv_(s, -1))
                    PE.transpose(bank[4 + n][:, 0:P], hd[n], ident[:]).then_inc(t_full[2], 1)
                s = earlier(t, 3)
                n = s[1] % 2
                if in_range(s, 0, NTILE):
                    e = pe.value_load(tab[0:1, bass.ds(index(s) + P, 1)], min_val=0, max_val=NE - 1)
                    pe.wait_ge(hT_done, tv_(s, 1))
                    if s[0] is not None or s[1] >= 2:
                        pe.wait_ge(yb_done, tv_(s, -1))
                    PE.matmul(bank[6 + n][:, 0:D], hT[n], wdn[:, bass.ds(e * D, D)], start=True, stop=True)\
                        .then_inc(t_full[3], 1)

            in_fours(tile, NTILE, pe, 3)


def constants():
    import numpy as np
    theta = np.float32(1.0) / np.float32(10000.0) ** (np.arange(0, DH, 2, dtype=np.float32) / np.float32(DH))
    ang = np.arange(T, dtype=np.float32)[:, None] * theta[None, :]
    ang = np.concatenate([ang, ang], axis=-1)
    c, s = np.cos(ang), np.sin(ang)
    s[:, :DH // 2] *= -1
    scale = np.array([DH ** -0.5, 1.0], np.float32)[None, :, None]

    def tiles(a):
        a = (a[:, None, :] * scale).reshape(TT, P, 2, DH)
        return np.ascontiguousarray(a.transpose(1, 0, 2, 3), dtype=np.float32)

    above = np.stack([np.triu(np.ones((P, P), np.float32), 1), np.ones((P, P), np.float32)], axis=1)
    e = np.arange(NE, dtype=np.float32)[None, :]
    p = np.arange(P, dtype=np.float32)[:, None]
    rows = np.stack([e + 0 * p, e * REG + 0 * p, p + 0 * e, 1 + 0 * e + 0 * p], axis=1).astype(np.float32)
    return tiles(c), tiles(s), np.eye(P, dtype=np.float32), above, rows


_INS = ['x', 'x_txt', 'L0_tok_log_dt', 'L0_tok_inv_A_real', 'L0_tok_A_imag', 'L0_tok_B_ri', 'L0_txt_W', 'L0_txt_b',
        'L0_attn_w_qkv', 'L0_attn_w_out', 'L0_attn_b_out', 'L0_ffn_router_w', 'L0_ffn_router_bias',
        'L0_ffn_up_proj', 'L0_ffn_gate_proj', 'L0_ffn_down_proj', 'L0_ffn_sh_gate', 'L0_ffn_sh_up',
        'L0_ffn_sh_down']


def kernel(**inputs):
    import numpy as np
    import concourse.bacc as bacc
    from concourse.bass_utils import run_bass_kernel_spmd

    nc = bacc.Bacc("TRN2", target_bir_lowering=False, num_devices=1)
    arrays, args = {}, []
    for name, a in [(n, inputs[n]) for n in _INS] + list(zip(("rope_cos", "rope_sin", "identity", "prefix", "expert_rows"), constants())):
        a = np.ascontiguousarray(a)
        arrays[f"in_{name}_dram"] = a
        args.append(nc.dram_tensor(f"in_{name}_dram", a.shape, mybir.dt.from_np(a.dtype), kind="ExternalInput").ap())
    out = nc.dram_tensor("out_dram", (NB, T, D), mybir.dt.float32, kind="ExternalOutput").ap()
    build(nc, *args, out)
    r = run_bass_kernel_spmd(nc, [arrays], core_ids=[0])
    return r.results[0]["out_dram"]
```

```python
import concourse.bass as bass
from concourse import mybir
from contextlib import ExitStack
import math

P = 128
NB = 16
D = 256
NS = 256
N = 64
NT = 128
T = NS + NT
TT = T // P
VOCAB = 50257
NH, DH = 16, 16
QW = 64
QR = 3 * DH
NE = 16
ED = 128
EPS = 1e-5
ROOTS = 12
SPLIT = -4096
LOG2E = 1.4426950408889634
ROUND = 12582912.0
LN2_HI, LN2_LO = 0.693359375, -2.12194440e-4
EXP_TERMS = 7
MAGIC = 1597463007.0
LA = 4
LB = D // LA
HC = 32
NCH = P // HC
SP_TOK = 56
SP_LEAD = 8
TU = 8

TOPK = 2
SLOTS = TT * TOPK
REG = NB * T + P
XROWS = NE * REG + P
NTILE = NB * T * TOPK // P + NE
ROWS_AT = 9
OWN = "DVE works the table out from counts, and none of its values can lie outside"
TG = 4
PAR_STEPS = 30
WT_STEP = PAR_STEPS + 1
POST_STEPS = 23
OUT_STEPS = 3 + 20 + 6 + 2 + 4
LN_STEPS = 20 + 1

F_READS = [1, 1] + [1] * 3 + [3] * 3 + [1, 1, 2, 2] * 3
O_READS = [1] * 13 + [2] + [1] * 4
X_USE, V_USE, QK_USE, SPLIT_USE = 0, 2, 5, 8
NORM_USE, ATT_USE, PROJ_USE, X2_USE, ROUTE_USE, FFN_USE, RANK_USE, DOWN_USE = 0, 3, 5, 8, 10, (11, 14), 13, 16


def reads(uses, u, n):
    return sum(uses[n:u:2])


def val(b, per, c, step=2):
    i, off = b
    return off * per + c if i is None else i * (step * per) + (off * per + c)


def is_batch(b, n):
    return b[0] is None and b[1] == n


def batch_index(b):
    i, off = b
    return off if i is None else i * 2 + off


def half(b, per):
    i, off = b
    return (off // 2 + 1) * per if i is None else i * per + (off // 2 + 1) * per


class Steps:

    def __init__(self, eng, sem, per):
        self.eng, self.sem, self.per = eng, sem, per

    def start(self, b):
        self.b, self.k = b, 0

    def add(self, ins):
        self.k += 1
        ins.then_inc(self.sem, 1)

    def done(self):
        self.eng.wait_ge(self.sem, val(self.b, self.per, self.k))

    def __call__(self, ins):
        self.add(ins)
        self.done()

    def end(self):
        assert self.k == self.per, (self.k, self.per)


def build(nc, x, x_txt, log_dt, inv_A_real, A_imag, B_ri, txt_W, txt_b, w_qkv, w_out, b_out,
          router_w, router_bias, up_proj, gate_proj, down_proj, sh_gate, sh_up, sh_down,
          rope_cos, rope_sin, identity, prefix, expert_rows, out):
    f32, f32r, bf16, i32, u32 = (mybir.dt.float32, mybir.dt.float32r, mybir.dt.bfloat16, mybir.dt.int32,
                                 mybir.dt.uint32)
    ALU, ACT, AX = mybir.AluOpType, mybir.ActivationFunctionType, mybir.AxisListType
    V, S, PE = nc.vector, nc.scalar, nc.tensor

    ctx = ExitStack()
    with ctx:
        def sb(name, shape, dt=f32):
            return ctx.enter_context(nc.sbuf_tensor(name, shape, dt))

        def sem(name):
            return ctx.enter_context(nc.semaphore(name))

        text_d = nc.dram_tensor("text_d", (NB * NT, D), f32, kind="Internal").ap()
        x_d = nc.dram_tensor("x_d", (XROWS, D), f32, kind="Internal").ap()
        y_d = nc.dram_tensor("y_d", (NTILE * P, D), f32, kind="Internal").ap()
        h2_d = nc.dram_tensor("h2_d", (NB, T, D), f32, kind="Internal").ap()
        kern_d = nc.dram_tensor("kern_d", (P, 2, NB, D), f32, kind="Internal").ap()

        ident = sb("ident", [P, P])
        wqkv = sb("wqkv", [P, 2, 3 * D])
        wout = sb("wout", [P, 2, D])
        shg_t, shu_t, shd_t = (sb(n, [P, 2, D]) for n in ("shg_t", "shu_t", "shd_t"))
        rw_t = sb("rw_t", [P, 2, NE])
        cos = sb("cos", [P, TT, 2, DH])
        sin = sb("sin", [P, TT, 2, DH])
        bout = sb("bout", [P, D])
        btxt = sb("btxt", [P, D])
        rbias = sb("rbias", [P, NE])
        ids = sb("ids", [1, NB * NT], i32)
        topv = sb("topv", [P, NB * TT, 2])
        pos_all = sb("pos_all", [P, NB * SLOTS])
        ef_all = sb("ef_all", [P, NB * SLOTS])
        pfx = sb("pfx", [P, 2, P])
        erow = sb("erow", [P, 4, NE])
        tabc = sb("tabc", [P, 2])
        tab = sb("tab", [1, 2 * P], i32)
        ends = sb("ends", [P, NE], i32)
        pw = sb("pw", [P, NB * TT, TOPK])
        tv = sb("tv", [P, TT, 8])
        ti = sb("ti", [P, TT, 8], u32)

        gbuf = [sb(f"gbuf{n}", [P, TT, D]) for n in range(2)]
        hres = [sb(f"hres{n}", [P, TT, D]) for n in range(2)]
        xn = sb("xn", [P, TT, D])
        xnT = sb("xnT", [P, 2, T])
        attn = sb("attn", [P, TT, D])
        attnT = sb("attnT", [P, 2, T])
        h1 = sb("h1", [P, TT, D])
        xn2 = sb("xn2", [P, TT, D])
        xn2T = sb("xn2T", [P, 2, T])
        h2 = sb("h2", [P, TT, D])
        hid = sb("hid", [P, 2, T])
        ra = sb("ra", [P, 2 * NH, DH])
        rb = sb("rb", [P, 2 * NH, DH])
        rc = sb("rc", [P, 2 * NH, DH])
        tu, tg = (r[:, :, :].rearrange("p h d -> p (h d)")[:, 0:T] for r in (ra, rb))
        rs = sb("rs", [P, TT, NH])
        ef = sb("ef", [P, SLOTS])
        oh = sb("oh", [P, SLOTS, NE])
        ohb = sb("ohb", [P, SLOTS + 1, NE], bf16)
        pfx_b = sb("pfx_b", [P, 2, P], bf16)
        rk = sb("rk", [P, SLOTS, NE])
        cum = sb("cum", [P, NE])
        posf = sb("posf", [P, SLOTS])
        pos = sb("pos", [P, SLOTS], u32)
        lg = sb("lg", [P, TT, NE])
        bst = sb("bst", [P, TT, 6])
        mv = sb("mv", [P, TT, 2])
        nwt = sb("nwt", [P, 4, TT])
        factor, shift = sb("factor", [P, TT]), sb("shift", [P, TT])
        mx = sb("mx", [P, TT, P // NH, NH])
        mxT = sb("mxT", [P, T], f32r)
        pick = sb("pick", [P, NH], f32r)

        at = [0]

        def take(words, pattern, **kw):
            a = arena[:, at[0]:at[0] + words].rearrange(pattern, **kw)
            at[0] += words
            return a

        with nc.sbuf_tensor("ssm_arena", [P, 32512], f32) as arena:
            xin = take(NB * 2 * 2 * N, "p (c s w) -> p c s w", c=NB, s=2)
            CB = [take(NB * P, "p (c h) -> p c h", c=NB) for _ in range(2)]
            PW = take(9 * 2 * P, "p (k r h) -> p k r h", k=9, r=2)
            VV = [[take(HC * LB, "p (h b) -> p h b", h=HC) for _ in range(2)] for _ in range(2)]
            CC = [[take(HC * NB * LA, "p (h c a) -> p h c a", h=HC, c=NB) for _ in range(2)] for _ in range(2)]
            TM = [take(HC * LB // 2, "p (h b) -> p h b", h=HC) for _ in range(4)]
            KS = [take(512, "p (h b) -> p h b", h=8) for _ in range(3)]
            KS.append(hid[:, :, :].rearrange("p e t -> p (e t)")[:, 0:512].rearrange("p (h b) -> p h b", h=8))
            assert at[0] <= 32512
        weights_words = TT * 2 * NH * QW + 8 * T + NH * T
        with ExitStack() as attention:
            st = attention.enter_context(nc.sbuf_tensor("st", [P, TT, 2, NH, QW], f32))
            QT, KT, VP = [], [], []
            for n in range(2):
                QT.append(attention.enter_context(nc.sbuf_tensor(f"QT{n}", [P, 8, T], f32r)))
                KT.append(attention.enter_context(nc.sbuf_tensor(f"KT{n}", [P, NH, T], f32r)))
            for n in range(2):
                VP.append(attention.enter_context(nc.sbuf_tensor(f"VP{n}", [P, TT, NH, 32], f32)))
            EX = attention.enter_context(nc.sbuf_tensor("EX", [P, 6, T], f32))
            OT = attention.enter_context(nc.sbuf_tensor("OT", [P, 4, T], f32))
        arena = ctx.enter_context(nc.sbuf_tensor("moe_arena", [P, 32512], f32))
        at[0] = 0
        wgu = take(2 * NE * 2 * ED, "p (k m) -> p k m", k=2)
        wdn = take(NE * D, "p (m) -> p m")
        assert at[0] <= weights_words
        at[0] = weights_words
        xb = [take(D, "p (d) -> p d") for _ in range(TG)]
        yb = [take(D, "p (d) -> p d") for _ in range(TG)]
        xT = [take(D, "p (k t) -> p k t", k=2) for _ in range(2)]
        th, sg, hd, hT = ([take(ED, "p (e) -> p e") for _ in range(2)] for _ in range(4))
        ya = [[take(D, "p (d) -> p d") for _ in range(TOPK)] for _ in range(TG)]
        hb = [take(D, "p (d) -> p d") for _ in range(TG)]
        ob = [take(D, "p (d) -> p d") for _ in range(TG)]
        hb2 = [take(D, "p (d) -> p d") for _ in range(TG)]
        zero = take(D, "p (d) -> p d")
        ohall = take(NB * SLOTS * NE, "p (j e) -> p j e", e=NE)
        posy = take(NB * SLOTS, "p (j) -> p j")
        assert at[0] <= 32512
        pr = [sb(f"pr{n}", [P, TOPK], u32) for n in range(TG)]
        prm = h1[:, :, :].rearrange("p t d -> p (t d)")
        ldt, iA, Ai = prm[:, 126:128], prm[:, 128:256], prm[:, 256:384]
        expin = prm[:, 126:256]
        Bi = prm[:, 384:640].rearrange("p (m r) -> p m r", r=2)
        zt = xn2[:, :, :].rearrange("p t d -> p (t d)")
        zz = [zt[:, P * n:P * (n + 1)] for n in range(6)]
        wT = attn[:, 0:2, :].rearrange("p t (k h) -> p (t k) h", h=P)
        shraw = [gbuf[0][:, 0:2, :], gbuf[1][:, 0:2, :], hres[0][:, 0:2, :]]
        rwraw = hres[1][0:NE, 0, :]

        bank = [ctx.enter_context(nc.psum_tensor(f"bank{n}", [P, 512], f32)) for n in range(8)]
        BS, BP, BM = bank[0:4], bank[4:6], bank[6:8]

        s_par = sem("s_par")
        s_x = sem("s_x")
        s_ident = sem("s_ident")
        s_const = sem("s_const")
        s_shw = sem("s_shw")
        s_ids = sem("s_ids")
        pre_dve = sem("pre_dve")
        pre_tr = sem("pre_tr")
        w_tr = sem("w_tr")
        pre_ev = sem("pre_ev")
        cb_done = sem("cb_done")
        chunk_dve = sem("chunk_dve")
        chunk_ready = sem("chunk_ready")
        chunk_a0 = sem("chunk_a0")
        kern_full = sem("kern_full")
        kern_ev = sem("kern_ev")
        kern_st = [sem(f"kern_st{n}") for n in range(4)]
        presets = sem("presets")
        text_sp = [sem(f"text_sp{n}") for n in range(2)]
        text_pool = [sem(f"text_pool{n}") for n in range(2)]
        rows_in = [sem(f"rows_in{n}") for n in range(2)]
        g_used = sem("g_used")
        d_ln = sem("d_ln")
        d_rope = sem("d_rope")
        d_out = sem("d_out")
        xn_ready = sem("xn_ready")
        st_ready = sem("st_ready")
        m_full = sem("m_full")
        m_read = [sem(f"m_read{n}") for n in range(2)]
        a_full = sem("a_full")
        a_read = sem("a_read")
        mxt_done = sem("mxt_done")
        stat_ready = sem("stat_ready")
        b_full = sem("b_full")
        max_ready = sem("max_ready")
        exp_done = sem("exp_done")
        pv_done = sem("pv_done")
        ot_ready = sem("ot_ready")
        xn2_ready = sem("xn2_ready")
        tanh_done = sem("tanh_done")
        h2_out = sem("h2_out")
        oh_ready = sem("oh_ready")
        pos_ready = sem("pos_ready")
        x_scat = sem("x_scat")
        post_dve = sem("post_dve")
        tab_full = sem("tab_full")
        tails = sem("tails")
        w_exp = sem("w_exp")
        pw_exp = sem("pw_exp")
        x_in = [sem(f"x_in{n}") for n in range(TG)]
        t_full = [sem(f"t_full{n}") for n in range(4)]
        xT_done, th_done, hT_done = sem("xT_done"), sem("th_done"), sem("hT_done")
        sg_done, hd_done, yb_done = sem("sg_done"), sem("hd_done"), sem("yb_done")
        y_out = [sem(f"y_out{n}") for n in range(TG)]
        pr_done = sem("pr_done")
        y_in = [sem(f"y_in{n}") for n in range(TG)]
        h_in = [sem(f"h_in{n}") for n in range(TG)]
        mix1, mix2 = sem("mix1"), sem("mix2")
        passed = {eng: sem(f"passed_{n}") for eng, n in ((nc.sync, "sp"), (nc.gpsimd, "pool"), (nc.vector, "dve"))}
        out_st = [sem(f"out_st{n}") for n in range(TG)]

        def parts_value(part, b, f, o, c):
            if part == "F":
                return c if is_batch(b, 0) else val(b, f + o, c - o)
            return val(b, f + o, c + (f if is_batch(b, NB - 1) else 2 * f))

        def filled(part, b, u):
            return parts_value(part, b, len(F_READS), len(O_READS), u + 1)

        def was_read(part, b, u, n):
            return parts_value(part, b, reads(F_READS, len(F_READS), n), reads(O_READS, len(O_READS), n),
                               reads(F_READS if part == "F" else O_READS, u, n))

        def wait_filled(eng, part, b, u):
            eng.wait_ge(m_full, filled(part, b, u))

        def wait_read(eng, part, b, first, last):
            for u in range(max(first, last - 1), last + 1):
                eng.wait_ge(m_read[u % 2], was_read(part, b, u + 1, u % 2))

        def wait(eng, s, v):
            if not isinstance(v, int) or v > 0:
                eng.wait_ge(s, v)

        def pass_on(eng):
            eng.sem_inc(passed[eng], 1)

        O_AT = {0: ["norm"], 1: ["attnT"], 2: ["proj"], 9: ["xn2T"], 10: ["router", "ffn0"], 11: ["rank"],
                12: ["ffn1"], 13: ["down"]}
        ROOT_AT = 3
        F1_AT = {14: ["xnT"], 15: ["v-0", "v-1", "v-2"]}
        F2_AT = {-1: ["qk-0", "residual"], 1: ["qk-1"], 3: ["qk-2"], **{s: [f"split-{s - 4}"] for s in range(4, 16)}}

        def all_of(*tables):
            return [name for table in tables for names in table.values() for name in names]

        def stage(name):
            kind, _, n = name.partition("-")
            return kind, int(n or 0)

        def in_pairs(batch, eng, peeled=1):
            for off in range(2 * peeled):
                batch((None, off))
            with eng.Fori(peeled, NB // 2 - 1) as i:
                for off in (0, 1):
                    batch((i, off))
            for off in (NB - 2, NB - 1):
                batch((None, off))

        def in_fours(tile, count, eng, behind=0):
            for off in range(TG):
                tile((None, off))
            with eng.Fori(1, count // TG) as i:
                for off in range(TG):
                    tile((i, off))
            for off in range(count, count + behind):
                tile((None, off))

        def earlier(t, n):
            return t[0], t[1] - n

        def index(t):
            i, off = t
            return off if i is None else i * TG + off

        def tv_(t, c):
            return val(t, 1, c, TG)

        def ring(t, c=1):
            i, off = t
            return 16 * c * (off // TG + 1) if i is None else i * (16 * c) + 16 * c * (off // TG + 1)

        def in_range(t, lo, hi):
            return t[0] is not None or lo <= t[1] < hi

        def gather(eng, b, first, count, signal):
            i, off = b
            if first in (0, SP_TOK):
                if not (is_batch(b, 0) or is_batch(b, 1)):
                    eng.wait_ge(signal[off % 2], half((i, off - 2), 16 * (SP_TOK if first == 0 else NT - SP_TOK)))
                    pass_on(eng)
            eng.wait_ge(s_ids, 16)
            with eng.Fori(0, count // TU) as j:
                at_ = [j * TU + (batch_index(b) * NT + first + n) for n in range(TU)]
                _, cols = nc.values_load_multi_w_load_instructions(ids[0:1, bass.ds(at_[0], TU)], [eng.engine], min_val=0, max_val=VOCAB - 1)
                for t, col in zip(at_, cols):
                    eng.dma_start(text_d[bass.ds(t, 1), :], txt_W[:, bass.ds(col, 1)].rearrange("h o -> o h"),
                                  allow_slow_non_contiguous=True).then_inc(signal[off % 2], 16)

        def zero_tails(eng, first):
            _, rows = nc.values_load_multi_w_load_instructions(ends[0:1, first * NE // 2:(first + 1) * NE // 2],
                                                               [eng.engine], min_val=0, max_val=NE * REG - P,
                                                               skip_runtime_bounds_check_because=OWN)
            for r in rows:
                eng.dma_start(x_d[bass.ds(r, P), :], zero).then_inc(tails, 16)

        def store_kernel(act, u):
            act.wait_ge(kern_full, u + 1)
            if u >= 4:
                act.wait_ge(kern_st[u % 4], 16 * (u // 4))
            S.copy(KS[u % 4], bank[u % 8][:, :].rearrange("p (h b) -> p h b", h=8)).then_inc(kern_ev, 1)
            act.wait_ge(kern_ev, u + 1)
            dst = kern_d[8 * u:8 * u + 8, :, :, :].rearrange("h s c (a b) -> (s c a) h b", a=LA)
            act.dma_start(dst, KS[u % 4]).then_inc(kern_st[u % 4], 16)

        def store_out(act, b):
            wait_read(act, "O", b, DOWN_USE, DOWN_USE + 1)
            dst = h2_d[bass.ds(batch_index(b), 1), :, :].rearrange("o (t p) d -> p (o t) d", p=P)
            act.dma_start(dst, h2[:]).then_inc(h2_out, 16)

        block = ctx.enter_context(nc.Block())

        @block.sync
        def _(sp):
            two = "(k p) n -> p k n"
            sp.dma_start(ldt, log_dt.rearrange("(s p) -> p s", p=P), allow_slow_non_contiguous=True).then_inc(s_par, 16)
            sp.dma_start(iA.rearrange("p (s n) -> p s n", s=2), inv_A_real.rearrange("(s p) n -> p s n", p=P)).then_inc(s_par, 16)
            sp.dma_start(Ai.rearrange("p (s n) -> p s n", s=2), A_imag.rearrange("(s p) n -> p s n", p=P)).then_inc(s_par, 16)
            sp.dma_start(prm[:, 384:640].rearrange("p (s m) -> p s m", s=2),
                         B_ri.rearrange("(s p) n r -> p s (n r)", p=P)).then_inc(s_par, 16)
            sp.dma_start(ident[:], identity).then_inc(s_ident, 16)
            sp.dma_start(ids[:], x_txt.rearrange("b t -> (b t)").unsqueeze(0)).then_inc(s_ids, 16)
            for c in range(0, NB, 4):
                for s in range(2):
                    sp.dma_start(xin[:, c:c + 4, s, :],
                                 x[c:c + 4, s * P:(s + 1) * P, :, :].rearrange("c p n r -> p c (n r)")).then_inc(s_x, 16)
            for raw, src in zip(shraw, (sh_gate, sh_up, sh_down)):
                sp.dma_start(raw, src.rearrange(two, p=P)).then_inc(s_shw, 16)
            sp.dma_start(rwraw, router_w).then_inc(s_shw, 16)
            sp.dma_start(wqkv[:], w_qkv.rearrange(two, p=P)).then_inc(s_const, 16)
            sp.dma_start(wout[:], w_out.rearrange(two, p=P)).then_inc(s_const, 16)
            sp.dma_start(cos[:], rope_cos).then_inc(s_const, 16)
            sp.dma_start(sin[:], rope_sin).then_inc(s_const, 16)
            sp.dma_start(bout[:], b_out.partition_broadcast(P)).then_inc(s_const, 16)
            sp.dma_start(btxt[:], txt_b.partition_broadcast(P)).then_inc(s_const, 16)
            sp.dma_start(pfx[:], prefix).then_inc(s_const, 16)
            sp.dma_start(erow[:], expert_rows).then_inc(s_const, 16)
            sp.dma_start(rbias[:], router_bias.partition_broadcast(P)).then_inc(s_const, 16)

            def load(b):
                i, off = b
                par = off % 2
                sp.wait_ge(text_sp[par], half(b, 16 * SP_TOK))
                pass_on(sp)
                sp.wait_ge(text_pool[par], half(b, 16 * (NT - SP_TOK)))
                wait(sp, g_used, val(b, 1, -1))
                pass_on(sp)
                c = batch_index(b)
                if is_batch(b, 0):
                    for n in range(4):
                        sp.wait_ge(kern_st[n], 64)
                    sp.wait_ge(w_tr, 4)
                sp.dma_start(gbuf[par][:, 0:2, :],
                             kern_d[:, :, bass.ds(c, 1), :].rearrange("p s o l -> p s (o l)")).then_inc(rows_in[par], 16)
                sp.dma_start(gbuf[par][:, 2, :], text_d[bass.ds(c * NT, NT), :]).then_inc(rows_in[par], 16)

            sp.wait_ge(s_ids, 16)

            def batch(b):
                gather(sp, b, 0, SP_LEAD, text_sp)
                if is_batch(b, 2):
                    load((None, 0))
                    load((None, 1))
                elif not (is_batch(b, 0) or is_batch(b, 1)):
                    load((b[0], b[1] - 1))
                gather(sp, b, SP_LEAD, SP_TOK - SP_LEAD, text_sp)

            in_pairs(batch, sp, 2)
            load((None, NB - 1))

            sp.wait_ge(post_dve, POST_STEPS)
            sp.wait_ge(x_scat, 16 * SLOTS * NB)
            sp.dma_start(x_d[NE * REG:XROWS, :], zero).then_inc(tails, 16)
            zero_tails(sp, 0)
            sp.wait_ge(pw_exp, 2)
            sp.wait_ge(tails, 16 * (NE + 1))

            def tile(t):
                if in_range(t, 0, NTILE):
                    if not in_range(t, 0, TG) or t[0] is not None:
                        sp.wait_ge(t_full[0], tv_(t, 1 - TG))
                    _, (r,) = nc.values_load_multi_w_load_instructions(
                        tab[0:1, bass.ds(index(t), 1)], [sp.engine], min_val=0, max_val=XROWS - P,
                        skip_runtime_bounds_check_because=OWN)
                    sp.dma_start(xb[t[1] % TG], x_d[bass.ds(r, P), :]).then_inc(x_in[t[1] % TG], 16)

            in_fours(tile, NTILE, sp)
            sp.wait_ge(h2_out, 16 * NB)

            def mix(t):
                if t[0] is not None:
                    sp.wait_ge(mix1, tv_(t, 1 - TG))
                sp.dma_start(hb[t[1] % TG], h2_d.rearrange("b t d -> (b t) d")[bass.ds(index(t) * P, P), :])\
                    .then_inc(h_in[t[1] % TG], 16)

            in_fours(mix, NB * TT, sp)
            for n in range(TG):
                sp.wait_ge(out_st[n], 16 * NB * TT // TG)

        @block.gpsimd
        def _(pool):
            pool.wait_ge(s_ids, 16)
            def scatter(b):
                pool.wait_ge(pos_ready, val(b, 1, 1))
                pass_on(pool)
                for j in range(SLOTS):
                    pool.indirect_dma_start(x_d[:, :], bass.IndirectOffsetOnAxis(ap=pos[:, j:j + 1], axis=0),
                                            xn2[:, j // TOPK, :], None).then_inc(x_scat, 16)

            def batch(b):
                gather(pool, b, SP_TOK, NT - SP_TOK, text_pool)
                if not any(is_batch(b, n) for n in range(3)):
                    scatter((b[0], b[1] - 3))

            in_pairs(batch, pool, 2)
            scatter((None, NB - 3))
            scatter((None, NB - 2))
            scatter((None, NB - 1))

            def store(t):
                pool.wait_ge(yb_done, tv_(t, 1))
                pass_on(pool)
                pool.dma_start(y_d[bass.ds(index(t) * P, P), :], yb[t[1] % TG]).then_inc(y_out[t[1] % TG], 16)

            in_fours(store, NTILE, pool)
            for n in range(TG):
                pool.wait_ge(y_out[n], 16 * NTILE // TG)

            def mix(t):
                pool.wait_ge(pr_done, tv_(t, 1))
                pass_on(pool)
                for k in range(TOPK):
                    pool.indirect_dma_start(ya[t[1] % TG][k], None, y_d[:, :],
                                            bass.IndirectOffsetOnAxis(ap=pr[t[1] % TG][:, k:k + 1], axis=0))\
                        .then_inc(y_in[t[1] % TG], 16)

            in_fours(mix, NB * TT, pool)

        @block.scalar
        def _(act):
            for n, dst in enumerate((shg_t, shu_t, shd_t)):
                act.wait_ge(w_tr, n + 1)
                S.copy(dst[:, :, :].rearrange("p k n -> p (k n)"), bank[n][:]).then_inc(pre_ev, 1)
            act.wait_ge(w_tr, 4)
            S.copy(rw_t[:, :, :].rearrange("p k n -> p (k n)"), bank[3][:, 0:2 * NE]).then_inc(pre_ev, 1)
            for q in range(NCH):
                act.wait_ge(cb_done, NB // 4)
                if q >= 2:
                    act.wait_ge(kern_full, 4 * (q - 1))
                for r, sign in ((0, 1.0), (1, -1.0)):
                    S.activation(CC[q % 2][r][:, :, :, 0],
                                 CB[r][:, :, q * HC:(q + 1) * HC].rearrange("p c h -> p h c"),
                                 ACT.Copy, scale=sign).then_inc(chunk_a0, 1)
                if q >= 1:
                    for u in range(4 * (q - 1), 4 * q):
                        store_kernel(act, u)
            for u in range(4 * (NCH - 1), 4 * NCH):
                store_kernel(act, u)

            def v_copy(b, t):
                par = b[1] % 2
                u = V_USE + t
                wait_filled(act, "F", b, u)
                if t == 0:
                    wait(act, pv_done, val(b, NH, -NH))
                S.copy(VP[par][:, t, :, 0:DH], BM[u % 2][:, 0:D].rearrange("p (h d) -> p h d", h=NH))\
                    .then_inc(m_read[u % 2], 1)

            def f_stage(b, name):
                par = b[1] % 2
                kind, t = stage(name)
                if kind == "xnT":
                    transposed(b, "F", X_USE, xnT)
                elif kind == "v":
                    v_copy(b, t)
                elif kind == "split":
                    u = SPLIT_USE + t
                    cols = slice(t // 4 * P, (t // 4 + 1) * P)
                    n = t % 2
                    wait_filled(act, "F", b, u)
                    if t % 4 < 2:
                        S.copy(QT[par][:, 4 * n:4 * n + 4, cols],
                               BM[n][:, :].rearrange("p (c q) -> p c q", c=4)).then_inc(m_read[n], 1)
                    else:
                        for odd in range(2):
                            rows = slice(64 * odd, 64 * odd + 64)
                            S.copy(KT[par][rows, 8 * n + odd:8 * n + 8:2, cols],
                                   BM[n][rows, :].rearrange("p (c q) -> p c q", c=4)).then_inc(m_read[n], 1)

            def transposed(b, part, u, dst):
                for k in range(2):
                    wait_filled(act, part, b, u + k)
                    S.copy(dst[:, k, :], BM[(u + k) % 2][:, 0:T]).then_inc(m_read[(u + k) % 2], 1)

            def o_stage(b, name):
                if name == "attnT":
                    transposed(b, "O", ATT_USE, attnT)
                elif name == "xn2T":
                    act.wait_ge(stat_ready, val(b, 2, 2))
                    wait(act, x_scat, val(b, 16 * SLOTS, 0))
                    for t in range(TT):
                        S.activation(xn2[:, t, :], h1[:, t, :], ACT.Identity, scale=factor[:, t:t + 1],
                                     bias=shift[:, t:t + 1]).then_inc(xn2_ready, 1)
                    transposed(b, "O", X2_USE, xn2T)
                elif name in ("ffn0", "ffn1"):
                    u = FFN_USE[int(name[-1])]
                    wait_filled(act, "O", b, u)
                    S.activation(tg, BM[u % 2][:, 0:T], ACT.Tanh, scale=0.5).then_inc(tanh_done, 1)

            def h1_half(b, o_b, f_b):
                for s in range(NH):
                    for name in O_AT.get(s, []) if o_b else []:
                        o_stage(o_b, name)
                    for name in F1_AT.get(s, []) if f_b else []:
                        f_stage(f_b, name)
                act.wait_ge(a_full, val(b, 49, 49))
                S.copy(mxT[:, :], BS[0][:, 0:T]).then_inc(mxt_done, 1)
                if o_b:
                    store_out(act, o_b)

            def h2_half(b, f_b):
                for name in F2_AT[-1] if f_b else []:
                    f_stage(f_b, name)
                for s in range(NH):
                    for t in range(TT):
                        u = TT * s + t
                        act.wait_ge(b_full, val(b, 48, u + 1))
                        wait(act, pv_done, val(b, NH, s - 1))
                        S.activation(EX[:, u % 6, :], BS[u % 4][:, 0:T], ACT.Exp).then_inc(exp_done, 1)
                    for name in F2_AT.get(s, []) if f_b else []:
                        f_stage(f_b, name)

            act.wait_ge(presets, 7)
            for name in all_of(F1_AT):
                f_stage((None, 0), name)
            act.wait_ge(presets, 9)
            for name in all_of(F2_AT):
                f_stage((None, 0), name)

            def batch(b):
                i, off = b
                if is_batch(b, NB - 1):
                    for n, w in enumerate((gate_proj, up_proj)):
                        for k in range(2):
                            dst = wgu[:, k, :].rearrange("p (e n m) -> p e n m", e=NE, n=2)[:, :, n, :]
                            act.dma_start(dst, w[:, k * P:(k + 1) * P, :].rearrange("e p m -> p e m")).then_inc(w_exp, 16)
                    act.dma_start(wdn.rearrange("p (e d) -> p e d", e=NE),
                                  down_proj.rearrange("e p d -> p e d")).then_inc(w_exp, 16)
                h1_half(b, None if is_batch(b, 0) else (i, off - 1),
                        None if is_batch(b, NB - 1) else (i, off + 1))
                h2_half(b, None if is_batch(b, NB - 1) else (i, off + 1))

            in_pairs(batch, act)
            for name in all_of(O_AT):
                o_stage((None, NB - 1), name)
            store_out(act, (None, NB - 1))

            act.wait_ge(post_dve, 2)
            S.activation(pw[:, :, 1], pw[:, :, 0], ACT.Exp).then_inc(pw_exp, 1)
            act.wait_ge(post_dve, POST_STEPS)
            act.wait_ge(x_scat, 16 * SLOTS * NB)
            zero_tails(act, 1)
            act.wait_ge(tab_full, 1)
            S.copy(tab[:, :], bank[0][0:1, 0:2 * P]).then_inc(pw_exp, 1)

            def tile(t):
                n = t[1] % 2
                if in_range(t, 0, NTILE):
                    act.wait_ge(t_full[0], tv_(t, 1))
                    S.copy(xT[n].rearrange("p k t -> p (k t)"), bank[n][:, 0:D]).then_inc(xT_done, 1)
                s = earlier(t, 1)
                if in_range(s, 0, NTILE):
                    act.wait_ge(t_full[1], tv_(s, 1))
                    S.activation(th[s[1] % 2], bank[2 + s[1] % 2][:, 0:ED], ACT.Tanh, scale=0.5).then_inc(th_done, 1)
                s = earlier(t, 2)
                if in_range(s, 0, NTILE):
                    act.wait_ge(t_full[2], tv_(s, 1))
                    S.copy(hT[s[1] % 2], bank[4 + s[1] % 2][:, 0:ED]).then_inc(hT_done, 1)

            in_fours(tile, NTILE, act, 3)

            def mix(t):
                act.wait_ge(mix2, tv_(t, 1))
                dst = out.rearrange("b t d -> (b t) d")[bass.ds(index(t) * P, P), :]
                act.dma_start(dst, ob[t[1] % TG]).then_inc(out_st[t[1] % TG], 16)

            in_fours(mix, NB * TT, act)

        @block.vector
        def _(dve):
            TM0 = [t.rearrange("p h b -> p (h b)")[:, 0:P] for t in TM]
            pre = Steps(dve, pre_dve, 10**6)
            pre.start((None, 0))

            def cmul(step, re, im, ur, ui, fr, fi, tmp, neg=False):
                step.add(V.tensor_tensor(tmp[0], ur, fr, ALU.mult))
                step.add(V.tensor_tensor(tmp[1], ui, fi, ALU.mult))
                step.add(V.tensor_tensor(tmp[2], ur, fi, ALU.mult))
                step(V.tensor_tensor(tmp[3], ui, fr, ALU.mult))
                step.add(V.tensor_tensor(re, tmp[0], tmp[1], ALU.subtract))
                if neg:
                    step(V.scalar_tensor_tensor(im, tmp[2], -1.0, tmp[3], ALU.mult, ALU.subtract))
                else:
                    step(V.tensor_tensor(im, tmp[2], tmp[3], ALU.add))

            dve.wait_ge(s_par, 64)
            xe, ne_, re_, qe = (zt[:, 192 * n:192 * n + 130] for n in range(4))
            pre(V.tensor_scalar(xe, expin, -87.0, 88.0, ALU.max, ALU.min))
            pre(V.tensor_scalar(ne_, xe, LOG2E, ROUND, ALU.mult, ALU.add))
            pre(V.tensor_scalar(ne_, ne_, ROUND, None, ALU.subtract))
            pre(V.scalar_tensor_tensor(re_, ne_, -LN2_HI, xe, ALU.mult, ALU.add))
            pre(V.scalar_tensor_tensor(re_, ne_, -LN2_LO, re_, ALU.mult, ALU.add))
            pre.add(V.tensor_scalar(xe.bitcast(i32), ne_, 127.0, float(1 << 23), ALU.add, ALU.mult))
            pre(V.tensor_scalar(qe, re_, 1.0 / math.factorial(EXP_TERMS), None, ALU.mult))
            for k in range(EXP_TERMS - 1, 0, -1):
                pre(V.scalar_tensor_tensor(qe, qe, 1.0 / math.factorial(k), re_, ALU.add, ALU.mult))
            pre(V.scalar_tensor_tensor(expin, qe, 1.0, xe, ALU.add, ALU.mult))
            dt_ = ldt
            zr, zi, t0, t1, t2, t3 = zz
            for s in range(2):
                cs_ = slice(s * N, (s + 1) * N)
                pre.add(V.tensor_scalar(zr[:, cs_], iA[:, cs_], dt_[:, s:s + 1], -0.5, ALU.mult, ALU.mult))
                pre(V.tensor_scalar(zi[:, cs_], Ai[:, cs_], dt_[:, s:s + 1], 0.5, ALU.mult, ALU.mult))
            pre.add(V.tensor_tensor(t0, zr, zr, ALU.mult))
            pre.add(V.tensor_tensor(t1, zi, zi, ALU.mult))
            pre(V.tensor_scalar(t2, zr, -1.0, 1.0, ALU.mult, ALU.add))
            pre.add(V.tensor_tensor(t2, t2, t2, ALU.mult))
            pre(V.tensor_tensor(t3, t0, t1, ALU.add))
            pre(V.tensor_tensor(t2, t2, t1, ALU.add))
            pre.add(V.tensor_scalar(t3, t3, -1.0, 1.0, ALU.mult, ALU.add))
            pre(V.reciprocal(t2, t2))
            pre.add(V.tensor_tensor(t0, t3, t2, ALU.mult))
            pre(V.scalar_tensor_tensor(t1, zi, 2.0, t2, ALU.mult, ALU.mult))
            pre.add(V.tensor_scalar(zr, Bi[:, :, 0], 2.0, None, ALU.mult))
            pre(V.tensor_scalar(zi, Bi[:, :, 1], 2.0, None, ALU.mult))
            assert pre.k == PAR_STEPS, pre.k
            dve.wait_ge(pre_tr, 1)
            pre(V.tensor_copy(wT, bank[4][:, :].rearrange("p (k h) -> p k h", h=P)))
            assert pre.k == WT_STEP
            pre.add(V.tensor_copy(PW[:, 0, :, :], wT[:, 0:2, :]))
            pre.done()
            for k in range(7):
                a, c = PW[:, k, 0, :], PW[:, k, 1, :]
                pre.add(V.tensor_tensor(TM0[0], a, a, ALU.mult))
                pre.add(V.tensor_tensor(TM0[1], c, c, ALU.mult))
                pre(V.scalar_tensor_tensor(PW[:, k + 1, 1, :], a, 2.0, c, ALU.mult, ALU.mult))
                pre(V.tensor_tensor(PW[:, k + 1, 0, :], TM0[0], TM0[1], ALU.subtract))
            cmul(pre, PW[:, 8, 0, :], PW[:, 8, 1, :], PW[:, 6, 0, :], PW[:, 6, 1, :],
                 PW[:, 7, 0, :], PW[:, 7, 1, :], TM0)
            for g in range(NB // 4):
                dve.wait_ge(pre_tr, 2 + g)
                pair = (4, 5) if g % 2 == 0 else (6, 7)
                ur, ui = (bank[n][:, :].rearrange("p (c h) -> p c h", c=4) for n in pair)
                br, bi = (wT[:, 2 + r, :].unsqueeze(1).to_broadcast([P, 4, P]) for r in range(2))
                tmp = [t.rearrange("p h b -> p (h b)")[:, 0:512].rearrange("p (c h) -> p c h", c=4) for t in TM]
                cmul(pre, CB[0][:, 4 * g:4 * g + 4, :], CB[1][:, 4 * g:4 * g + 4, :], ur, ui, br, bi, tmp)
                dve.sem_inc(cb_done, 1)

            ck = Steps(dve, chunk_dve, 10**6)
            ck.start((None, 0))
            for q in range(NCH):
                hp = slice(q * HC, (q + 1) * HC)
                vr, vi = VV[q % 2]
                cr, ci = CC[q % 2]
                if q >= 2:
                    dve.wait_ge(kern_full, 4 * (q - 1))
                ck.add(V.memset(vr[:, :, 0:1], 1.0))
                ck.add(V.memset(vi[:, :, 0:1], 0.0))
                ck.add(V.tensor_copy(vr[:, :, 1], PW[:, 0, 0, hp]))
                ck(V.tensor_copy(vi[:, :, 1], PW[:, 0, 1, hp]))
                for k in range(1, 6):
                    w = 1 << k
                    fr, fi = (PW[:, k, r, hp].unsqueeze(2).to_broadcast([P, HC, w]) for r in range(2))
                    tmp = [t[:, :, 0:w] for t in TM]
                    cmul(ck, vr[:, :, w:2 * w], vi[:, :, w:2 * w], vr[:, :, 0:w], vi[:, :, 0:w], fr, fi, tmp)
                br, bi = (CB[r][:, :, hp].rearrange("p c h -> p h c") for r in range(2))
                for a in range(1, LA):
                    fr, fi = (PW[:, 5 + a, r, hp].unsqueeze(2).to_broadcast([P, HC, NB]) for r in range(2))
                    tmp = [t[:, :, 0:NB] for t in TM]
                    cmul(ck, cr[:, :, :, a], ci[:, :, :, a], br, bi, fr, fi, tmp, neg=True)
                dve.sem_inc(chunk_ready, 1)

            dve.wait_ge(kern_ev, 16)
            for n in range(4):
                dve.wait_ge(kern_st[n], 64)
            dve.wait_ge(s_const, 16 * 9)
            ps = Steps(dve, presets, 10**6)
            ps.start((None, 0))
            V.memset(st[:, :, :, :, QR:QW].rearrange("p t s h w -> p (t s h) w"), 0.0).then_inc(chunk_dve, 1)
            for n in range(2):
                V.memset(VP[n][:, :, :, DH:32].rearrange("p t h w -> p (t h) w"), 0.0).then_inc(chunk_dve, 1)
            dve.wait_ge(chunk_dve, ck.k + 3)
            V.tensor_tensor(pick[:, :], ident[:, 0:NH], ident[:, NH:2 * NH], ALU.add).then_inc(presets, 1)
            for n in range(2):
                V.memset(VP[n][:, :, :, DH], 1.0).then_inc(presets, 1)
            V.memset(mx[:, :, :, :], 0.0).then_inc(presets, 1)
            V.tensor_copy(cum[:, :], erow[:, 1, :]).then_inc(presets, 1)
            V.memset(ohb[:, SLOTS, :], 0.0).then_inc(presets, 1)
            V.tensor_copy(pfx_b[:, :, :], pfx[:]).then_inc(presets, 1)
            dve.wait_ge(presets, 7)

            ln = Steps(dve, d_ln, LN_STEPS)
            ro = Steps(dve, d_rope, TT * 3)
            ou = Steps(dve, d_out, OUT_STEPS)

            v, y, hv, t_ = (nwt[:, n, :] for n in range(4))

            def moments(step, src):
                for t in range(TT):
                    step.add(V.bn_stats(bst[:, t, :], src[:, t, :]))
                step.done()
                step.add(V.memset(nwt[:, :, :], 0.0))
                for t in range(TT):
                    step.add(V.bn_aggr(mv[:, t, :], bst[:, t, :]))
                step.done()

            def root(step, k):
                step.done()
                if k == 0:
                    step.add(V.tensor_scalar(v, mv[:, :, 1], EPS, None, ALU.add))
                elif k == 1:
                    step.add(V.tensor_scalar(hv, v, -0.5, None, ALU.mult))
                    step.add(V.tensor_scalar(t_.bitcast(i32), v.bitcast(i32), 1, None, ALU.logical_shift_right))
                elif k == 2:
                    step.add(V.tensor_scalar(y.bitcast(i32), t_.bitcast(i32), -1.0, MAGIC, ALU.mult, ALU.add))
                elif k % 3 == 0:
                    step.add(V.tensor_tensor(t_, y, y, ALU.mult))
                elif k % 3 == 1:
                    step.add(V.tensor_tensor(t_, t_, hv, ALU.mult))
                else:
                    step.add(V.scalar_tensor_tensor(y, t_, 1.5, y, ALU.add, ALU.mult))

            def rope(b, t):
                par = b[1] % 2
                if t == 0:
                    ro.start(b)
                u = QK_USE + t
                wait_filled(dve, "F", b, u)
                qk = BM[u % 2][:, :].rearrange("p (s h d) -> p s h d", s=2, h=NH)
                sh = [P, 2, NH, DH]
                a4, b4, c4 = (r[:, :, :].rearrange("p (s h) d -> p s h d", s=2) for r in (ra, rb, rc))
                cs = cos[:, t, :, :].unsqueeze(2).to_broadcast(sh)
                sn = sin[:, t, :, :].unsqueeze(2).to_broadcast(sh)
                V.tensor_tensor(a4, qk, cs, ALU.mult).then_inc(m_read[u % 2], 1)
                hd = DH // 2
                for f in range(2):
                    o = slice(f * hd, f * hd + hd)
                    i_ = slice((1 - f) * hd, (1 - f) * hd + hd)
                    V.tensor_tensor(b4[:, :, :, o], qk[:, :, :, i_], sn[:, :, :, o], ALU.mult).then_inc(m_read[u % 2], 1)
                wait_read(dve, "F", b, u, u)
                ro(V.tensor_tensor(rc[:, :, :], ra[:, :, :], rb[:, :, :], ALU.add))
                q_, k_ = st[:, t, 0, :, :], st[:, t, 1, :, :]
                for s, dst, step in ((0, q_, 2), (1, k_, 1)):
                    rep = dst[:, :, 0:QR].rearrange("p h (n d) -> p h n d", d=DH)[:, :, 0:3:step, :] if step == 2 \
                        else dst[:, :, 0:2 * DH].rearrange("p h (n d) -> p h n d", d=DH)
                    src = rc[:, NH * s:NH * (s + 1), :].unsqueeze(2).to_broadcast([P, NH, 2, DH])
                    ro.add(V.tensor_scalar(rep.bitcast(i32), src.bitcast(i32), SPLIT, None, ALU.bitwise_and))
                ro.done()
                V.tensor_tensor(q_[:, :, DH:2 * DH], rc[:, 0:NH, :], q_[:, :, 0:DH], ALU.subtract)\
                    .then_inc(st_ready, 1)
                V.tensor_tensor(k_[:, :, 2 * DH:3 * DH], rc[:, NH:2 * NH, :], k_[:, :, 0:DH], ALU.subtract)\
                    .then_inc(st_ready, 1)
                dve.wait_ge(st_ready, val(b, 2 * TT, 2 * t + 2))
                if t == TT - 1:
                    ro.end()

            def f_stage(b, name):
                par = b[1] % 2
                kind, t = stage(name)
                if kind == "rows":
                    ln.start(b)
                    g = gbuf[par]
                    dve.wait_ge(rows_in[par], half(b, 32))
                    ln(V.tensor_tensor(g[:, 2, :], g[:, 2, :], btxt[:], ALU.add))
                    moments(ln, g)
                    for k in range(ROOTS):
                        root(ln, k)
                    ln.done()
                    for t in range(TT):
                        V.tensor_scalar(xn[:, t, :], g[:, t, :], mv[:, t, 0:1], y[:, t:t + 1],
                                        ALU.subtract, ALU.mult).then_inc(xn_ready, 1)
                    ln.end()
                elif kind == "residual":
                    V.tensor_tensor(hres[par][:], gbuf[par][:], bout[:].unsqueeze(1).to_broadcast([P, TT, D]), ALU.add)\
                        .then_inc(g_used, 1)
                elif kind == "qk":
                    rope(b, t)

            def o_stage(b, name):
                par = b[1] % 2
                if name == "norm":
                    ou.start(b)
                    for t in range(TT):
                        u = NORM_USE + t
                        wait_filled(dve, "O", b, u)
                        o4 = BM[u % 2][:, :].rearrange("p (h w) -> p h w", h=NH)
                        ou(V.reciprocal(rs[:, t, :], o4[:, :, DH]))
                        V.tensor_tensor(attn[:, t, :].rearrange("p (h d) -> p h d", h=NH), o4[:, :, 0:DH],
                                        rs[:, t, :].unsqueeze(2).to_broadcast([P, NH, DH]), ALU.mult)\
                            .then_inc(m_read[u % 2], 1)
                elif name == "proj":
                    for t in range(TT):
                        u = PROJ_USE + t
                        wait_filled(dve, "O", b, u)
                        V.tensor_tensor(h1[:, t, :], BM[u % 2][:, 0:D], hres[par][:, t, :], ALU.add)\
                            .then_inc(m_read[u % 2], 1)
                    wait_read(dve, "O", b, PROJ_USE, PROJ_USE + 2)
                    moments(ou, h1)
                elif name.startswith("root"):
                    k = stage(name)[1]
                    root(ou, k)
                    if k == ROOTS - 1:
                        ou.done()
                        V.scalar_tensor_tensor(shift[:], mv[:, :, 0], -1.0, y, ALU.mult, ALU.mult)\
                            .then_inc(stat_ready, 1)
                        V.tensor_copy(factor[:], y).then_inc(stat_ready, 1)
                elif name == "router":
                    u = ROUTE_USE
                    wait_filled(dve, "O", b, u)
                    V.tensor_tensor(lg[:], BM[u % 2][:, 0:TT * NE].rearrange("p (t e) -> p t e", t=TT),
                                    rbias[:].unsqueeze(1).to_broadcast([P, TT, NE]), ALU.add)\
                        .then_inc(m_read[u % 2], 1)
                    wait_read(dve, "O", b, u, u)
                    pass_on(dve)
                    c = batch_index(b) * TT
                    for t in range(TT):
                        ou.add(V.max(tv[:, t, :], lg[:, t, :]))
                    ou.done()
                    pass_on(dve)
                    for t in range(TT):
                        ou.add(V.max_index(ti[:, t, :], tv[:, t, :], lg[:, t, :]))
                    ou.done()
                    ou.add(V.tensor_copy(topv[:, bass.ds(c, TT), :], tv[:, :, 0:TOPK]))
                    ou(V.tensor_copy(ef[:, :].rearrange("p (t k) -> p t k", k=TOPK), ti[:, :, 0:TOPK]))
                    sh = [P, SLOTS, NE]
                    V.tensor_tensor(oh[:], erow[:, 0:1, :].to_broadcast(sh), ef[:, :].unsqueeze(2).to_broadcast(sh),
                                    ALU.is_equal).then_inc(oh_ready, 1)
                    dve.wait_ge(oh_ready, val(b, 2, 1))
                    V.tensor_copy(ohb[:, 0:SLOTS, :], oh[:]).then_inc(oh_ready, 1)
                elif name == "rank":
                    u = RANK_USE
                    ps = BM[u % 2][:, 0:(SLOTS + 1) * NE].rearrange("p (j e) -> p j e", e=NE)
                    wait_filled(dve, "O", b, u)
                    r0 = was_read("O", b, u, u % 2)
                    V.tensor_tensor(rk[:], ps[:, 0:SLOTS, :], cum[:, :].unsqueeze(1).to_broadcast([P, SLOTS, NE]),
                                    ALU.add).then_inc(m_read[u % 2], 1)
                    dve.wait_ge(m_read[u % 2], r0 + 1)
                    V.tensor_tensor(cum[:, :], ps[:, SLOTS, :], cum[:, :], ALU.add).then_inc(m_read[u % 2], 1)
                    wait_read(dve, "O", b, u, u)
                    ou(V.tensor_tensor(rk[:], rk[:], oh[:], ALU.mult))
                    ou(V.tensor_reduce(posf[:], rk[:], AX.X, ALU.add))
                    ou.add(V.tensor_copy(pos_all[:, bass.ds(batch_index(b) * SLOTS, SLOTS)], posf[:]))
                    ou.add(V.tensor_copy(ef_all[:, bass.ds(batch_index(b) * SLOTS, SLOTS)], ef[:]))
                    V.tensor_copy(pos[:], posf[:]).then_inc(pos_ready, 1)
                    dve.wait_ge(pos_ready, val(b, 1, 1))
                    ou.done()
                    ou.end()
                elif name in ("ffn0", "ffn1"):
                    e = int(name[-1])
                    u = FFN_USE[e]
                    dve.wait_ge(tanh_done, val(b, 2, e + 1))
                    V.scalar_tensor_tensor(tu, tg, 1.0, BM[u % 2][:, 0:T], ALU.add, ALU.mult)\
                        .then_inc(m_read[u % 2], 1)
                    wait_read(dve, "O", b, u, u)
                    wait_filled(dve, "O", b, u + 1)
                    V.scalar_tensor_tensor(hid[:, e, :], tu, 0.5, BM[(u + 1) % 2][:, 0:T], ALU.mult, ALU.mult)\
                        .then_inc(m_read[(u + 1) % 2], 1)
                    wait_read(dve, "O", b, u + 1, u + 1)
                elif name == "down":
                    wait(dve, h2_out, val(b, 16, 0))
                    for n, tiles in enumerate(((0, 2), (2, 3))):
                        u = DOWN_USE + n
                        wait_filled(dve, "O", b, u)
                        lo, hi = tiles
                        V.tensor_tensor(h2[:, lo:hi, :],
                                        BM[u % 2][:, 0:(hi - lo) * D].rearrange("p (t d) -> p t d", d=D),
                                        h1[:, lo:hi, :], ALU.add).then_inc(m_read[u % 2], 1)

            def h1_half(b, o_b, f_b):
                wait(dve, mxt_done, val(b, 1, 0))
                for s in range(NH):
                    for t in range(TT):
                        u = TT * s + t
                        dve.wait_ge(a_full, val(b, 49, u + 1))
                        V.tensor_reduce(mx[:, t, 1, s:s + 1], BS[u % 4][:, 0:T], AX.X, ALU.max)\
                            .then_inc(a_read, 1)
                        if o_b and ROOT_AT <= s < ROOT_AT + ROOTS // TT:
                            o_stage(o_b, f"root-{TT * (s - ROOT_AT) + t}")
                    for name in O_AT.get(s, []) if o_b else []:
                        o_stage(o_b, name)
                    for name in F1_AT.get(s, []) if f_b else []:
                        f_stage(f_b, name)
                dve.wait_ge(a_read, val(b, 49, 48))
                V.tensor_scalar(mx[:, :, 1, :], mx[:, :, 1, :], -1.0, None, ALU.mult).then_inc(a_read, 1)
                dve.wait_ge(a_read, val(b, 49, 49))
                V.tensor_scalar(mx[:, :, 0, :].bitcast(i32), mx[:, :, 1, :].bitcast(i32), SPLIT, None,
                                ALU.bitwise_and).then_inc(max_ready, 1)
                dve.wait_ge(max_ready, val(b, 2, 1))
                V.tensor_tensor(mx[:, :, 1, :], mx[:, :, 1, :], mx[:, :, 0, :], ALU.subtract).then_inc(max_ready, 1)

            def h2_half(b, f_b, rows_b):
                for name in F2_AT[-1] if f_b else []:
                    f_stage(f_b, name)
                for s in range(NH):
                    for name in F2_AT.get(s, []) if f_b else []:
                        f_stage(f_b, name)
                    if s % 4 == 1 and s > 1:
                        ot_copy(b, s // 4 - 1)
                    if s == ROWS_AT and rows_b:
                        f_stage(rows_b, "rows")
                ot_copy(b, 3)

            def ot_copy(b, g):
                dve.wait_ge(pv_done, val(b, NH, 4 * g + 4))
                V.tensor_copy(OT[:, g, :], BP[g % 2][:, 0:T]).then_inc(ot_ready, 1)

            f_stage((None, 0), "rows")
            for n in range(2):
                V.memset(KT[n][:, :, :].bitcast(f32), 0.0).then_inc(presets, 1)
            for name in all_of(F1_AT, F2_AT):
                f_stage((None, 0), name)
            f_stage((None, 1), "rows")

            def batch(b):
                i, off = b
                h1_half(b, None if is_batch(b, 0) else (i, off - 1),
                        None if is_batch(b, NB - 1) else (i, off + 1))
                h2_half(b, None if is_batch(b, NB - 1) else (i, off + 1),
                        None if is_batch(b, NB - 2) or is_batch(b, NB - 1) else (i, off + 2))

            in_pairs(batch, dve)
            for name in all_of(O_AT):
                o_stage((None, NB - 1), name)
                if name == "proj":
                    for k in range(ROOTS):
                        o_stage((None, NB - 1), f"root-{k}")

            po = Steps(dve, post_dve, 10**6)
            po.start((None, 0))
            po.add(V.memset(zero, 0.0))
            po(V.tensor_tensor(pw[:, :, 0], topv[:, :, 1], topv[:, :, 0], ALU.subtract))
            f = [rk[:, n, :] for n in range(SLOTS)]
            g = [oh[:, n, :] for n in range(SLOTS)]
            one = [posf[:, n:n + 1] for n in range(SLOTS)]
            last, tiles_, tend, tbeg, first = cum[:, :], f[0], f[1], f[2], f[3]
            po.add(V.tensor_copy(ends[:], last))
            po.add(V.tensor_copy(ef[:, 0:1], erow[:, 2, 0:1]))
            po(V.tensor_tensor(f[4], last, erow[:, 1, :], ALU.subtract))
            it = lg[:, 0, :].bitcast(i32)
            po(V.tensor_scalar(it, f[4], float(P - 1), None, ALU.add))
            po(V.tensor_scalar(it, it, P.bit_length() - 1, None, ALU.logical_shift_right))
            po(V.tensor_copy(tiles_, it))
            po(V.tensor_tensor_scan(tend, erow[:, 3, :], tiles_, 0.0, ALU.mult, ALU.add))
            po(V.tensor_tensor(tbeg, tend, tiles_, ALU.subtract))
            t_ = ef[:, 0:1]
            po.add(V.tensor_scalar(g[0], tbeg, t_, None, ALU.is_le))
            po.add(V.tensor_scalar(g[1], tend, t_, None, ALU.is_le))
            po(V.scalar_tensor_tensor(first, tbeg, -float(P), erow[:, 1, :], ALU.mult, ALU.add))
            po(V.tensor_tensor(g[2], g[0], g[1], ALU.subtract))
            po.add(V.tensor_tensor(g[3], g[2], first, ALU.mult))
            po.add(V.tensor_tensor(g[4], g[2], erow[:, 0, :], ALU.mult))
            po(V.tensor_reduce(one[0], g[2], AX.X, ALU.add))
            po.add(V.tensor_reduce(one[1], g[3], AX.X, ALU.add))
            po.add(V.tensor_reduce(tabc[:, 1:2], g[4], AX.X, ALU.add))
            po.add(V.tensor_scalar(one[2], one[0], t_, float(P), ALU.mult, ALU.mult))
            po(V.tensor_scalar(one[3], one[0], -1.0, 1.0, ALU.mult, ALU.add))
            po(V.tensor_tensor(one[1], one[1], one[2], ALU.add))
            po.add(V.scalar_tensor_tensor(tabc[:, 0:1], one[3], float(NE * REG), one[1], ALU.mult, ALU.add))
            po.done()
            assert po.k == POST_STEPS, po.k
            shp = [P, NB * SLOTS, NE]
            po(V.tensor_tensor(ohall, erow[:, 0:1, :].to_broadcast(shp), ef_all[:].unsqueeze(2).to_broadcast(shp), ALU.is_equal))
            po(V.tensor_tensor(ohall, ohall, first.unsqueeze(1).to_broadcast(shp), ALU.mult))
            po(V.tensor_reduce(ef_all[:], ohall, AX.X, ALU.add))
            po(V.tensor_tensor(posy.bitcast(u32), pos_all[:], ef_all[:], ALU.subtract))
            dve.wait_ge(pw_exp, 1)
            po(V.tensor_scalar(pw[:, :, 0], pw[:, :, 1], 1.0, None, ALU.add))
            po(V.reciprocal(pw[:, :, 0], pw[:, :, 0]))
            po(V.tensor_tensor(pw[:, :, 1], pw[:, :, 1], pw[:, :, 0], ALU.mult))

            def tile(t):
                s = earlier(t, 1)
                n = s[1] % 2
                if in_range(s, 0, NTILE):
                    dve.wait_ge(th_done, tv_(s, 1))
                    gate, up = bank[2 + n][:, 0:ED], bank[2 + n][:, ED:2 * ED]
                    V.scalar_tensor_tensor(sg[n], th[n], 1.0, gate, ALU.add, ALU.mult).then_inc(sg_done, 1)
                    dve.wait_ge(sg_done, tv_(s, 1))
                    V.scalar_tensor_tensor(hd[n], sg[n], 0.5, up, ALU.mult, ALU.mult).then_inc(hd_done, 1)
                s = earlier(t, 3)
                n = s[1] % 2
                if in_range(s, 0, NTILE):
                    dve.wait_ge(t_full[3], tv_(s, 1))
                    if not in_range(s, 0, TG) or s[0] is not None:
                        dve.wait_ge(y_out[s[1] % TG], ring(earlier(s, TG)))
                    V.tensor_copy(yb[s[1] % TG], bank[6 + n][:, 0:D]).then_inc(yb_done, 1)

            in_fours(tile, NTILE, dve, 3)

            def rows(t):
                V.tensor_copy(pr[t[1] % TG][:], posy.bitcast(u32)[:, bass.ds(index(t) * TOPK, TOPK)]).then_inc(pr_done, 1)

            def mix(t):
                n, c = t[1] % TG, index(t)
                dve.wait_ge(h_in[n], ring(t))
                dve.wait_ge(y_in[n], ring(t, TOPK))
                V.scalar_tensor_tensor(hb2[n], ya[n][0], pw[:, bass.ds(c, 1), 0], hb[n], ALU.mult, ALU.add)\
                    .then_inc(mix1, 1)
                dve.wait_ge(mix1, tv_(t, 1))
                if t[0] is not None or t[1] >= TG:
                    dve.wait_ge(out_st[n], ring(earlier(t, TG)))
                V.scalar_tensor_tensor(ob[n], ya[n][1], pw[:, bass.ds(c, 1), 1], hb2[n], ALU.mult, ALU.add)\
                    .then_inc(mix2, 1)

            def turn(t):
                s = earlier(t, TG - 1)
                if t[0] is not None or t[1] >= TG:
                    dve.wait_ge(mix2, tv_(t, 1 - TG))
                if in_range(t, 0, NB * TT):
                    rows(t)
                if in_range(s, 0, NB * TT):
                    mix(s)

            in_fours(turn, NB * TT, dve, TG - 1)

        @block.tensor
        def _(pe):
            pe.wait_ge(s_ident, 16)
            pe.wait_ge(pre_dve, PAR_STEPS)
            for n, src in enumerate((zz[2], zz[3], zz[0], zz[1])):
                ins = PE.transpose(bank[4][:, n * P:(n + 1) * P], src, ident[:])
            ins.then_inc(pre_tr, 1)
            pe.wait_ge(s_x, 16 * 8)
            for g in range(NB // 4):
                pair = (4, 5) if g % 2 == 0 else (6, 7)
                if g == 0:
                    pe.wait_ge(pre_dve, WT_STEP)
                if g >= 2:
                    pe.wait_ge(cb_done, g - 1)
                for c in range(4):
                    for r in range(2):
                        src = xin[:, 4 * g + c, :, :].rearrange("p s (n r) -> p (s n) r", r=2)[:, :, r]
                        ins = PE.transpose(bank[pair[r]][:, c * P:(c + 1) * P], src, ident[:])
                ins.then_inc(pre_tr, 1)
            pe.wait_ge(s_shw, 64)
            for n in range(3):
                for o in range(2):
                    for k in range(2):
                        ins = PE.transpose(bank[n][:, k * D + o * P:k * D + (o + 1) * P],
                                           shraw[n][:, o, k * P:(k + 1) * P], ident[:])
                ins.then_inc(w_tr, 1)
            for k in range(2):
                ins = PE.transpose(bank[3][:, k * NE:(k + 1) * NE], rwraw[:, k * P:(k + 1) * P], ident[0:NE, 0:NE])
            ins.then_inc(w_tr, 1)
            for u in range(16):
                q = u // 4
                if u % 4 == 0:
                    pe.wait_ge(chunk_ready, q + 1)
                    pe.wait_ge(chunk_a0, 2 * (q + 1))
                if u == 0:
                    pe.wait_ge(pre_ev, 4)
                if u == 4:
                    pe.wait_ge(cb_done, 4)
                if u >= 8:
                    pe.wait_ge(kern_ev, u - 7)
                for n in range(8):
                    hp = (u % 4) * 8 + n
                    for s in range(2):
                        rows = slice(64 * s, 64 * s + 64)
                        for r in range(2):
                            ins = PE.matmul(bank[u % 8][rows, n * LB:(n + 1) * LB],
                                            CC[q % 2][r][rows, hp, :, :].rearrange("p c a -> p (c a)"),
                                            VV[q % 2][r][rows, hp, :], start=(r == 0), stop=(r == 1),
                                            tile_position=(64 * s, 64 * s))
                ins.then_inc(kern_full, 1)

            def m_bank(part, b, u):
                wait(pe, m_read[u % 2], was_read(part, b, u, u % 2))
                return BM[u % 2]

            def rows_transposed(part, b, u, src):
                for k in range(2):
                    ps = m_bank(part, b, u + k)
                    for n in range(TT):
                        ins = PE.transpose(ps[:, n * P:(n + 1) * P], src[:, n, k * P:(k + 1) * P], ident[:])
                    ins.then_inc(m_full, 1)

            def f_stage(b, name):
                par = b[1] % 2
                kind, t = stage(name)
                if kind == "xnT":
                    pe.wait_ge(xn_ready, val(b, TT, TT))
                    rows_transposed("F", b, X_USE, xn)
                elif kind in ("v", "qk"):
                    wait_read(pe, "F", b, X_USE, X_USE + 1)
                    lo, hi = (0, 2 * D) if kind == "qk" else (2 * D, 3 * D)
                    ps = m_bank("F", b, (QK_USE if kind == "qk" else V_USE) + t)
                    for k in range(2):
                        ins = PE.matmul(ps[:, 0:hi - lo], xnT[:, k, t * P:(t + 1) * P], wqkv[:, k, lo:hi],
                                        start=(k == 0), stop=(k == 1))
                    ins.then_inc(m_full, 1)
                elif kind == "split":
                    tile, s, n = t // 4, t // 2 % 2, t % 2
                    pe.wait_ge(st_ready, val(b, 2 * TT, 2 * tile + 2))
                    ps = m_bank("F", b, SPLIT_USE + t)
                    for c in range(4):
                        src = st[:, tile, s, 8 * n + 2 * c:8 * n + 2 * c + 2, :].rearrange("p h w -> p (h w)")
                        ins = PE.transpose(ps[:, c * P:(c + 1) * P], src, ident[:])
                    ins.then_inc(m_full, 1)

            def o_stage(b, name):
                if name == "norm":
                    pe.wait_ge(ot_ready, val(b, 4, 4))
                    for t in range(TT):
                        ps = m_bank("O", b, NORM_USE + t)
                        for g in range(4):
                            ins = PE.transpose(ps[:, g * P:(g + 1) * P], OT[:, g, t * P:(t + 1) * P], ident[:])
                        ins.then_inc(m_full, 1)
                elif name == "attnT":
                    wait_read(pe, "O", b, NORM_USE, NORM_USE + 2)
                    rows_transposed("O", b, ATT_USE, attn)
                elif name == "proj":
                    wait_read(pe, "O", b, ATT_USE, ATT_USE + 1)
                    for t in range(TT):
                        ps = m_bank("O", b, PROJ_USE + t)
                        for k in range(2):
                            ins = PE.matmul(ps[:, 0:D], attnT[:, k, t * P:(t + 1) * P], wout[:, k, :],
                                            start=(k == 0), stop=(k == 1))
                        ins.then_inc(m_full, 1)
                elif name == "xn2T":
                    pe.wait_ge(xn2_ready, val(b, TT, TT))
                    rows_transposed("O", b, X2_USE, xn2)
                elif name == "router":
                    wait_read(pe, "O", b, X2_USE, X2_USE + 1)
                    ps = m_bank("O", b, ROUTE_USE)
                    for t in range(TT):
                        for k in range(2):
                            ins = PE.matmul(ps[:, t * NE:(t + 1) * NE], xn2T[:, k, t * P:(t + 1) * P], rw_t[:, k, :],
                                            start=(k == 0), stop=(k == 1))
                    ins.then_inc(m_full, 1)
                elif name == "rank":
                    pe.wait_ge(oh_ready, val(b, 2, 2))
                    ps = m_bank("O", b, RANK_USE)
                    PE.matmul(ps[:, 0:(SLOTS + 1) * NE], pfx_b[:, 0, :], ohb[:, :, :].rearrange("p j e -> p (j e)"),
                              start=True, stop=False)
                    for n in range(1, SLOTS + 1):
                        ins = PE.matmul(ps[:, n * NE:(SLOTS + 1) * NE], pfx_b[:, 1, :],
                                        ohb[:, 0:SLOTS + 1 - n, :].rearrange("p j e -> p (j e)"),
                                        start=False, stop=(n == SLOTS))
                    ins.then_inc(m_full, 1)
                elif name in ("ffn0", "ffn1"):
                    e = int(name[-1])
                    for n, w in enumerate((shg_t, shu_t)):
                        ps = m_bank("O", b, FFN_USE[e] + n)
                        for k in range(2):
                            ins = PE.matmul(ps[:, 0:T], w[:, k, e * P:(e + 1) * P], xn2T[:, k, :],
                                            start=(k == 0), stop=(k == 1))
                        ins.then_inc(m_full, 1)
                elif name == "down":
                    wait_read(pe, "O", b, FFN_USE[0] + 1, FFN_USE[1] + 1)
                    for t in range(TT):
                        if t != 1:
                            ps = m_bank("O", b, DOWN_USE + t // 2)
                        for k in range(2):
                            ins = PE.matmul(ps[:, (t % 2) * D:(t % 2 + 1) * D], hid[:, k, t * P:(t + 1) * P],
                                            shd_t[:, k, :], start=(k == 0), stop=(k == 1))
                        if t:
                            ins.then_inc(m_full, 1)

            def h1_half(b, o_b, f_b):
                par = b[1] % 2
                wait_read(pe, "F", b, SPLIT_USE, len(F_READS) - 1)
                for s in range(NH):
                    for t in range(TT):
                        u = TT * s + t
                        if u < 4:
                            wait(pe, exp_done, val(b, 48, u - 3))
                        else:
                            pe.wait_ge(a_read, val(b, 49, u - 3))
                        PE.matmul(BS[u % 4][:, 0:T], QT[par][:, s // 2, t * P:(t + 1) * P],
                                  KT[par][:, s, :], start=True, stop=True).then_inc(a_full, 1)
                    for name in O_AT.get(s, []) if o_b else []:
                        o_stage(o_b, name)
                    for name in F1_AT.get(s, []) if f_b else []:
                        f_stage(f_b, name)
                pe.wait_ge(max_ready, val(b, 2, 2))
                for t in range(TT):
                    ins = PE.transpose(BS[0][:, t * P:(t + 1) * P],
                                       mx[:, t, :, :].rearrange("p n h -> p (n h)"), ident[:])
                ins.then_inc(a_full, 1)

            def h2_half(b, f_b):
                par = b[1] % 2

                def pv(h, t):
                    g, j = h // 4, h % 4
                    if j == 0 and t == 0:
                        wait(pe, ot_ready, val(b, 4, g - 1))
                    pe.wait_ge(exp_done, val(b, 48, TT * h + t + 1))
                    ins = PE.matmul(BP[g % 2][32 * j:32 * j + 32, 0:T], VP[par][:, t, h, :],
                                    EX[:, (TT * h + t) % 6, :], start=(t == 0), stop=(t == TT - 1),
                                    tile_position=(0, 32 * j))
                    if t == TT - 1:
                        ins.then_inc(pv_done, 1)

                for name in F2_AT[-1] if f_b else []:
                    f_stage(f_b, name)
                pe.wait_ge(mxt_done, val(b, 1, 1))
                for s in range(NH):
                    for t in range(TT):
                        u = TT * s + t
                        if u >= 4:
                            pe.wait_ge(exp_done, val(b, 48, u - 3))
                        PE.matmul(BS[u % 4][:, 0:T], KT[par][:, s, t * P:(t + 1) * P],
                                  QT[par][:, s // 2, :], start=True, stop=False)
                        PE.matmul(BS[u % 4][:, 0:T], pick[:, s:s + 1].to_broadcast([P, P]), mxT[:, :],
                                  start=False, stop=True).then_inc(b_full, 1)
                        if s:
                            pv(s - 1, t)
                    for name in F2_AT.get(s, []) if f_b else []:
                        f_stage(f_b, name)
                for t in range(TT):
                    pv(NH - 1, t)

            for name in all_of(F1_AT, F2_AT):
                f_stage((None, 0), name)

            def batch(b):
                i, off = b
                h1_half(b, None if is_batch(b, 0) else (i, off - 1),
                        None if is_batch(b, NB - 1) else (i, off + 1))
                h2_half(b, None if is_batch(b, NB - 1) else (i, off + 1))

            in_pairs(batch, pe)
            for name in all_of(O_AT):
                o_stage((None, NB - 1), name)

            pe.wait_ge(post_dve, POST_STEPS)
            for n in range(2):
                ins = PE.transpose(bank[0][0:1, n * P:(n + 1) * P], tabc[:, n:n + 1], ident[:])
            ins.then_inc(tab_full, 1)
            pe.wait_ge(w_exp, 16 * 5)
            pe.wait_ge(pw_exp, 2)

            experts = {}

            def tile(t):
                n = t[1] % 2
                if in_range(t, 0, NTILE):
                    pe.wait_ge(x_in[t[1] % TG], ring(t))
                    if t[0] is not None or t[1] >= 2:
                        pe.wait_ge(xT_done, tv_(t, -1))
                    for k in range(2):
                        ins = PE.transpose(bank[n][:, k * P:(k + 1) * P], xb[t[1] % TG][:, k * P:(k + 1) * P], ident[:])
                    ins.then_inc(t_full[0], 1)
                if t[1] % TG == 0:
                    first = index(t) - 3 if t[0] is not None or t[1] else 0
                    last = min(t[1] + TG - 1, NTILE) if t[0] is None else None
                    count = TG + 2 if last is None else last - first
                    _, found = nc.values_load_multi_w_load_instructions(
                        tab[0:1, bass.ds(first + P, count)], [pe.engine], min_val=0, max_val=NE - 1,
                        skip_runtime_bounds_check_because=OWN)
                    base = -3 if t[0] is not None or t[1] else 0
                    experts.clear()
                    experts.update({t[1] + base + k: e for k, e in enumerate(found)})
                s = earlier(t, 1)
                n = s[1] % 2
                if in_range(s, 0, NTILE):
                    e = experts[s[1]]
                    pe.wait_ge(xT_done, tv_(s, 1))
                    if s[0] is not None or s[1] >= 2:
                        pe.wait_ge(hd_done, tv_(s, -1))
                    for k in range(2):
                        ins = PE.matmul(bank[2 + n][:, 0:2 * ED], xT[n][:, k, :],
                                        wgu[:, k, bass.ds(e * (2 * ED), 2 * ED)], start=(k == 0), stop=(k == 1))
                    ins.then_inc(t_full[1], 1)
                s = earlier(t, 2)
                n = s[1] % 2
                if in_range(s, 0, NTILE):
                    pe.wait_ge(hd_done, tv_(s, 1))
                    if s[0] is not None or s[1] >= 2:
                        pe.wait_ge(hT_done, tv_(s, -1))
                    PE.transpose(bank[4 + n][:, 0:P], hd[n], ident[:]).then_inc(t_full[2], 1)
                s = earlier(t, 3)
                n = s[1] % 2
                if in_range(s, 0, NTILE):
                    e = experts[s[1]]
                    pe.wait_ge(hT_done, tv_(s, 1))
                    if s[0] is not None or s[1] >= 2:
                        pe.wait_ge(yb_done, tv_(s, -1))
                    PE.matmul(bank[6 + n][:, 0:D], hT[n], wdn[:, bass.ds(e * D, D)], start=True, stop=True)\
                        .then_inc(t_full[3], 1)

            in_fours(tile, NTILE, pe, 3)


def constants():
    import numpy as np
    theta = np.float32(1.0) / np.float32(10000.0) ** (np.arange(0, DH, 2, dtype=np.float32) / np.float32(DH))
    ang = np.arange(T, dtype=np.float32)[:, None] * theta[None, :]
    ang = np.concatenate([ang, ang], axis=-1)
    c, s = np.cos(ang), np.sin(ang)
    s[:, :DH // 2] *= -1
    scale = np.array([DH ** -0.5, 1.0], np.float32)[None, :, None]

    def tiles(a):
        a = (a[:, None, :] * scale).reshape(TT, P, 2, DH)
        return np.ascontiguousarray(a.transpose(1, 0, 2, 3), dtype=np.float32)

    above = np.stack([np.triu(np.ones((P, P), np.float32), 1), np.ones((P, P), np.float32)], axis=1)
    e = np.arange(NE, dtype=np.float32)[None, :]
    p = np.arange(P, dtype=np.float32)[:, None]
    rows = np.stack([e + 0 * p, e * REG + 0 * p, p + 0 * e, 1 + 0 * e + 0 * p], axis=1).astype(np.float32)
    return tiles(c), tiles(s), np.eye(P, dtype=np.float32), above, rows


_INS = ['x', 'x_txt', 'L0_tok_log_dt', 'L0_tok_inv_A_real', 'L0_tok_A_imag', 'L0_tok_B_ri', 'L0_txt_W', 'L0_txt_b',
        'L0_attn_w_qkv', 'L0_attn_w_out', 'L0_attn_b_out', 'L0_ffn_router_w', 'L0_ffn_router_bias',
        'L0_ffn_up_proj', 'L0_ffn_gate_proj', 'L0_ffn_down_proj', 'L0_ffn_sh_gate', 'L0_ffn_sh_up',
        'L0_ffn_sh_down']


def kernel(**inputs):
    import numpy as np
    import concourse.bacc as bacc
    from concourse.bass_utils import run_bass_kernel_spmd

    nc = bacc.Bacc("TRN2", target_bir_lowering=False, num_devices=1)
    arrays, args = {}, []
    for name, a in [(n, inputs[n]) for n in _INS] + list(zip(("rope_cos", "rope_sin", "identity", "prefix", "expert_rows"), constants())):
        a = np.ascontiguousarray(a)
        arrays[f"in_{name}_dram"] = a
        args.append(nc.dram_tensor(f"in_{name}_dram", a.shape, mybir.dt.from_np(a.dtype), kind="ExternalInput").ap())
    out = nc.dram_tensor("out_dram", (NB, T, D), mybir.dt.float32, kind="ExternalOutput").ap()
    build(nc, *args, out)
    r = run_bass_kernel_spmd(nc, [arrays], core_ids=[0])
    return r.results[0]["out_dram"]
```
